# Optimizing a Trainium2 kernel written in Bass

```python
import numpy as np
import jax
import jax.numpy as jnp

def _softmax(x, axis=-1):
    return jax.nn.softmax(x, axis=axis)

def _gelu(x):
    return jax.nn.gelu(x, approximate=True)

def _silu(x):
    return jax.nn.silu(x)

def _sigmoid(x):
    return jax.nn.sigmoid(x)

def _layernorm(x, axis=-1, eps=1e-05):
    m = jnp.mean(x, axis=axis, keepdims=True)
    v = jnp.var(x, axis=axis, keepdims=True)
    return (x - m) / jnp.sqrt(v + eps)

def _scatter_add(tgt, idx, src, axis=0):
    return tgt.at[idx].add(src)

def _segment_sum(src, seg, n):
    return jax.ops.segment_sum(src, seg, n)
kernel_name = 'mk_seq_preln_d1_jaxref_r8_cfa376'

def setup_inputs(seed: int=0):
    np.random.seed(seed)
    _w = jnp.asarray

    def _L0_attn_setup():
        import jax, jax.numpy as jnp
        import numpy as np
        key = jax.random.key(seed)
        k1, k2, k3 = jax.random.split(key, 3)
        B, S, D, N = (2, 256, 128, 16)
        H = D // N
        x = jax.random.normal(k1, (B, S, D), dtype=jnp.float32)
        W_qkv = jax.random.normal(k2, (N, D, 3 * H), dtype=jnp.float32) / np.sqrt(D).astype(np.float32)
        W_out = jax.random.normal(k3, (N, H, D), dtype=jnp.float32) / np.sqrt(D).astype(np.float32)
        return {'x': x, 'W_qkv': W_qkv, 'W_out': W_out}
    _L0_attn_in = _L0_attn_setup()

    def _L0_ffn_setup():
        import jax, jax.numpy as jnp
        import numpy as np
        DIM = 128

        def _reference_tuple_inner(x, W_r, W_k, W_v, mu_r, mu_k):
            B, T, C = x.shape
            x_prev = jnp.concatenate([jnp.zeros((B, 1, C), x.dtype), x[:, :-1, :]], axis=1)
            xr = mu_r * x + (1.0 - mu_r) * x_prev
            xk = mu_k * x + (1.0 - mu_k) * x_prev
            r = jax.nn.sigmoid(jnp.einsum('btc,dc->btd', xr, W_r))
            k = jnp.einsum('btc,dc->btd', xk, W_k)
            k_act = jnp.square(jax.nn.relu(k))
            out = r * jnp.einsum('btc,dc->btd', k_act, W_v)
            new_state = x[:, -1, :]
            return (out, new_state)
        key = jax.random.key(seed)
        ks = jax.random.split(key, 6)
        B, T, C = (8, 256, DIM)
        x = jax.random.normal(ks[0], (B, T, C), dtype=jnp.float32)
        s = 1.0 / np.sqrt(C)
        W_r = jax.random.uniform(ks[1], (C, C), jnp.float32, -s, s)
        W_k = jax.random.uniform(ks[2], (C, C), jnp.float32, -s, s)
        W_v = jax.random.uniform(ks[3], (C, C), jnp.float32, -s, s)
        mu_r = jax.random.uniform(ks[4], (C,), jnp.float32)
        mu_k = jax.random.uniform(ks[5], (C,), jnp.float32)
        return {'x': x, 'W_r': W_r, 'W_k': W_k, 'W_v': W_v, 'mu_r': mu_r, 'mu_k': mu_k}
    _L0_ffn_in = _L0_ffn_setup()
    _d = {'L0_attn_x': _L0_attn_in['x'], 'L0_attn_W_qkv': _L0_attn_in['W_qkv'], 'L0_attn_W_out': _L0_attn_in['W_out'], 'L0_ffn_W_r': _L0_ffn_in['W_r'], 'L0_ffn_W_k': _L0_ffn_in['W_k'], 'L0_ffn_W_v': _L0_ffn_in['W_v'], 'L0_ffn_mu_r': _L0_ffn_in['mu_r'], 'L0_ffn_mu_k': _L0_ffn_in['mu_k']}
    _x0 = _d['L0_attn_x']
    _d['L0_attn_x'] = jax.random.normal(jax.random.fold_in(jax.random.key(seed), 1), (4, 1024, 128), dtype=_x0.dtype)
    del _x0
    return _d

def reference(L0_attn_x, L0_attn_W_qkv, L0_attn_W_out, L0_ffn_W_r, L0_ffn_W_k, L0_ffn_W_v, L0_ffn_mu_r, L0_ffn_mu_k):

    def _L0_attn_ref(x, W_qkv, W_out):
        import jax, jax.numpy as jnp
        import numpy as np
        B, S, D = x.shape
        head_dim = W_qkv.shape[-1] // 3
        qkv = jnp.einsum('bsd,ndh->bnsh', x, W_qkv)
        q, k, v = jnp.split(qkv, 3, axis=-1)
        scale = jnp.asarray(1.0 / np.sqrt(head_dim), dtype=x.dtype)
        attn = jnp.einsum('bnqh,bnkh->bnqk', q, k) * scale
        mask = jnp.asarray(-10000000000.0, dtype=x.dtype) * (1.0 - jnp.tril(jnp.ones((S, S), dtype=x.dtype)))
        attn = jax.nn.softmax(attn + mask, axis=-1)
        out = jnp.einsum('bnqk,bnkh->bnqh', attn, v)
        out = out.reshape(B, -1, S)
        return jnp.einsum('bds,nhd->bsd', out, W_out)

    def _L0_ffn_ref(x, W_r, W_k, W_v, mu_r, mu_k):
        import jax, jax.numpy as jnp
        import numpy as np
        DIM = 128

        def _reference_tuple_inner(x, W_r, W_k, W_v, mu_r, mu_k):
            B, T, C = x.shape
            x_prev = jnp.concatenate([jnp.zeros((B, 1, C), x.dtype), x[:, :-1, :]], axis=1)
            xr = mu_r * x + (1.0 - mu_r) * x_prev
            xk = mu_k * x + (1.0 - mu_k) * x_prev
            r = jax.nn.sigmoid(jnp.einsum('btc,dc->btd', xr, W_r))
            k = jnp.einsum('btc,dc->btd', xk, W_k)
            k_act = jnp.square(jax.nn.relu(k))
            out = r * jnp.einsum('btc,dc->btd', k_act, W_v)
            new_state = x[:, -1, :]
            return (out, new_state)
        return _reference_tuple_inner(x, W_r, W_k, W_v, mu_r, mu_k)[0]
    x = L0_attn_x
    x = x + _L0_attn_ref(_layernorm(x, axis=-1), L0_attn_W_qkv, L0_attn_W_out)
    x = x + _L0_ffn_ref(_layernorm(x, axis=-1), L0_ffn_W_r, L0_ffn_W_k, L0_ffn_W_v, L0_ffn_mu_r, L0_ffn_mu_k)
    return x

_drawn_inputs = setup_inputs


def setup_inputs(seed=0):
    import zlib

    import numpy as np

    out = dict(_drawn_inputs(seed))
    spreads = {}
    factors = {'L0_ffn_W_r': 3.171, 'L0_ffn_mu_r': 6.239}
    for name, (base, spread) in spreads.items():
        noise = np.random.default_rng([zlib.crc32(name.encode()), seed]).standard_normal(out[name].shape)
        drawn = base * np.exp(spread * noise) if base else spread * noise
        out[name] = jnp.asarray(drawn.astype(out[name].dtype))
    for name, factor in factors.items():
        out[name] = (out[name] * factor).astype(out[name].dtype)
    return out
```

```python
import concourse.bass as bass
import concourse.mybir as mybir
from contextlib import ExitStack

F32 = mybir.dt.float32
BF16 = mybir.dt.bfloat16
ALU = mybir.AluOpType
ACT = mybir.ActivationFunctionType
AX = mybir.AxisListType

B, S, D, N, H = 4, 1024, 128, 16, 8
T = S // 128
GH = 4
GROUPS = N // GH
HALF = S // 2
PARTS = 3
QK_ROWS = 96
ALL_ROWS = QK_ROWS + PARTS
VW = 32
CHUNKS = 36
AHEAD = 12
LAG = 3
RING = 3
PSLOTS = 12
SCALE = H ** -0.5
EPS = 1e-5
LOW = -1e30
QK_DMAS = 2 * PARTS * PARTS

def _pass2():
    chunks = []
    for half in range(2):
        base, t0 = half * HALF, half * 4
        for i in range(t0):
            chunks += [[(h, i, base, 512, 0)] for h in range(GH)]
        chunks += [[(h, t0, base, 512, 0)] for h in range(GH)]
        chunks += [[(h, t0 + 1, base + 128, 384, 0), (h, t0 + 3, base + 384, 128, 384)] for h in range(GH)]
        chunks += [[(h, t0 + 2, base + 256, 256, 256 * (h % 2)) for h in (p, p + 1)] for p in (0, 2)]
    return chunks


PASS2 = _pass2()
SET_ENDS = [3, 7, 9, 13, 17, 21, 25, 29, 33, 35]
SETS = len(SET_ENDS)
HALF_SETS = 3
DIAGONAL = {c: 0 for c in (0, 1, 2, 3, 26, 27, 28, 29)}
DIAGONAL |= {c: 3 for c in (4, 5, 6, 7, 30, 31, 32, 33)}
DIAGONAL |= {c: 2 for c in (8, 9, 34, 35)}
MASKS = len(DIAGONAL)


def masks_until(c):
    return sum(x <= c for x in DIAGONAL)


def set_of(c):
    return next(k for k, e in enumerate(SET_ENDS) if e >= c)


def pieces_of_set(k):
    first = SET_ENDS[k - 1] + 1 if k else 0
    found = {}
    for c in range(first, SET_ENDS[k] + 1):
        for h, i, q0, n, at in PASS2[c]:
            found.setdefault((i, q0, n), []).append((h, c, at))
    return [(i, q0, n, hs) for (i, q0, n), hs in found.items()]


def _pass1():
    chunks = [[(h, j, 0, 512, 0, None)] for j in range(4, 8) for h in range(GH)]
    chunks += [[(h, 3, 0, 512, 0, 384)] for h in range(GH)]
    chunks += [[(h, 7, 512, 512, 0, 384)] for h in range(GH)]
    for t0 in (0, 4):
        k0 = 128 * t0
        chunks += [[(h, t0, k0, 128, 0, 0), (h, t0 + 2, k0, 384, 128, 384)] for h in range(GH)]
    for t0 in (0, 4):
        k0 = 128 * t0
        chunks += [[(h, t0 + 1, k0, 256, 256 * (h % 2), 256 * (h % 2) + 128) for h in (p, p + 1)] for p in (0, 2)]
    return chunks


PASS1 = _pass1()

OT_LAST, OT_FIRST, MAX_ROW = ("out, 2nd half of the group before", 5), ("out, 1st half", 15), ("max", 26)
PROJECT = [("xT0", 17), ("xT1", 19), ("qk0", 21), ("qk1", 23), ("qk2", 28), ("qk3", 30), ("v0", 32), ("v1", 34)]
MIX = [("xT0", 20), ("xT1", 22), ("r0", 27), ("r1", 28), ("k0", 29), ("k1", 30), ("v0", 32), ("v1", 33), ("y0", 34), ("y1", 35)]
SETUP_USES = ["w_out", "w_t", "xT0", "xT1", "qk0", "qk1", "qk2", "qk3", "v0", "v1", "max"]


def uses_of(off, project, mix, first=False, last=False):
    uses = [] if first else [OT_LAST]
    uses += [OT_FIRST] + ([] if last else [MAX_ROW]) + (PROJECT if project else []) + (MIX if mix else [])
    uses.sort(key=lambda u: u[1])
    return {name: (n, step) for n, (name, step) in enumerate(uses)}


FIRST_USES = len(SETUP_USES) + 2
ROUND_USES = 11 + 3 + 3 + 13
USES_BEFORE = {0: -2, 1: 0, 2: 11, 3: 14, 4: 17}


class Phase:

    def __init__(self, i, off, project=False, mix=False, first=False, last=False, eng=None, products=None):
        self.i, self.off, self.project, self.mix = i, off, project, mix
        self.eng, self.products = eng, products
        self.first, self.last = first, last
        self.final = isinstance(i, int) and i == LAST_ROUND
        self.slot = off % GROUPS
        self.uses = uses_of(off, project, mix, first, last)
        self.steps = {step: name for name, (_, step) in self.uses.items()}
        self.before = {1: 0, 2: 3, 3: 6}[off] if self.final else USES_BEFORE[off]

    def per_round(self, each, more):
        if isinstance(self.i, int):
            return self.i * each + more
        if each not in self.products:
            self.products[each] = self.eng.snap(self.i * each)
        return self.products[each] + more

    def count(self, per_group, more):
        return self.per_round(GROUPS * per_group, self.off * per_group + more)

    def fills(self, ahead):
        return self.per_round(16 * QK_DMAS, 16 * QK_DMAS * ((self.off + ahead) // GROUPS + 1))

    def use(self, name):
        return self.per_round(ROUND_USES, FIRST_USES + self.before + self.uses[name][0])

    def first_pass(self, step):
        n = step + AHEAD
        ahead, r = 1 + n // CHUNKS, n % CHUNKS
        if self.last or (self.final and self.off + ahead >= GROUPS):
            return None
        return ahead, (self.off + ahead) % GROUPS, r


LAST_ROUND = B - 1


def build(nc, x, w_qkv, w_out, w_r, w_k, w_v, mu_r, mu_k, out):
    nc.disable_value_cache = True
    ctx = ExitStack()
    with ctx:
        def sb(name, shape, dt=F32):
            return ctx.enter_context(nc.sbuf_tensor(name, shape, dt))

        def ps(name):
            return ctx.enter_context(nc.psum_tensor(name, [128, 512], F32))

        def sem(name):
            return ctx.enter_context(nc.semaphore(name))

        qa = sb("qa", [128, GROUPS, GH, S], BF16)
        ka = sb("ka", [128, GROUPS, GH, S], BF16)
        va = sb("va", [128, GROUPS, T, GH, VW])
        probs = sb("probs", [128, PSLOTS, 512])
        q_parts = sb("q_parts", [128, PARTS, S], BF16)
        k_parts = sb("k_parts", [128, PARTS, S], BF16)
        v_all = sb("v_all", [128, T, D])
        x_ln = sb("x_ln", [128, T, D])
        x1 = sb("x1", [128, T, D])
        att = sb("att", [128, T, D])
        xn = sb("xn", [128, T, D])
        xT = sb("xT", [128, 1 + S])
        scaled = sb("scaled", [128, S])
        xr = sb("xr", [128, S])
        xk = sb("xk", [128, S])
        gate = sb("gate", [128, S])
        k_relu = sb("k_relu", [128, S])
        k_act = sb("k_act", [128, S])
        yT = sb("yT", [128, S])
        y = sb("y", [128, T, D])
        rest = sb("rest", [128, 2, 512])
        oT = sb("oT", [128, 512])
        inv = sb("inv", [128, 4, GH])
        inv_w = sb("inv_w", [128, 4, GH])
        part_max = sb("part_max", [128, GH, T, 3])
        far_max = sb("far_max", [128, GH, 4])
        q_max = sb("q_max", [128, GH * T])
        neg_rest = sb("neg_rest", [GH * T, 128])
        neg_parts = sb("neg_parts", [GH * T, PARTS, 128], BF16)
        stats = sb("stats", [128, T, 6])
        mean_var = sb("mean_var", [128, T, 2])
        var_eps = sb("var_eps", [128, T])
        rstd = sb("rstd", [128, T])
        shift = sb("shift", [128, T])
        minus_half = sb("minus_half", [128, T])
        w_all = sb("w_all", [128, N, 3 * H])
        wq = sb("wq", [128, D])
        wk = sb("wk", [128, D])
        wv = sb("wv", [128, D])
        wo = sb("wo", [128, D])
        w_sum = sb("w_sum", [128, D])
        w_mix = sb("w_mix", [128, 3, D])
        w_mixT = sb("w_mixT", [128, 3, D])
        mu = sb("mu", [128, 2])
        one_less_mu = sb("one_less_mu", [128, 2])
        ident = sb("ident", [128, 128])
        ident_bf = sb("ident_bf", [128, 128], BF16)
        causal = sb("causal", [128, 128], BF16)
        ones = sb("ones", [128, 128])

        bank2 = [ps(f"scores2_{n}") for n in range(RING)]
        bank1 = [ps(f"scores1_{n}") for n in range(RING)]
        acc = ps("acc")
        shared = ps("shared")

        x_in = sem("x_in")
        w_in = sem("w_in")
        x1_in = sem("x1_in")
        qk_in = [sem(f"qk_in{n}") for n in range(GROUPS)]
        rows_in = sem("rows_in")
        out_done = sem("out_done")
        pool_setup = sem("pool_setup")
        consts_ready = sem("consts_ready")
        zeroed = sem("zeroed")
        w_ready = sem("w_ready")
        bn_done = sem("bn_done")
        stats_ready = sem("stats_ready")
        norm_step = sem("norm_step")
        xn_ready = sem("xn_ready")
        bank_full = sem("bank_full")
        bank_read = sem("bank_read")
        hi_ready = sem("hi_ready")
        mid_ready = sem("mid_ready")
        lo_ready = sem("lo_ready")
        v_ready = sem("v_ready")
        s1_full = sem("s1_full")
        s1_read = sem("s1_read")
        far_done = sem("far_done")
        max_ready = sem("max_ready")
        split_step = sem("split_step")
        parts_ready = sem("parts_ready")
        s2_full = sem("s2_full")
        exp_done = sem("exp_done")
        masked = sem("masked")
        sets_done = sem("sets_done")
        acc_read = sem("acc_read")
        inv_step = sem("inv_step")
        att_ready = sem("att_ready")
        scaled_r = sem("scaled_r")
        mixed = sem("mixed")
        gate_ready = sem("gate_ready")
        act_ready = sem("act_ready")
        y_ready = sem("y_ready")

        values_cleared = sem("values_cleared")
        pool_passed = sem("pool_passed")
        dve_passed = sem("dve_passed")

        block = ctx.enter_context(nc.Block())

        def wait_apart(eng, sem, value):
            eng.wait_ge(sem, value)
            if not isinstance(value, int):
                eng.sem_inc(pool_passed if eng is nc.gpsimd else dve_passed, 1)

        def rounds(eng, phase):
            phase(Phase(0, 0, first=True))
            with eng.Fori(0, B - 1) as i:
                multiples = {}
                phase(Phase(i, 1, project=True, eng=eng, products=multiples))
                phase(Phase(i, 2, eng=eng, products=multiples))
                phase(Phase(i, 3, eng=eng, products=multiples))
                phase(Phase(i, 4, mix=True, eng=eng, products=multiples))
            for off in (1, 2, 3):
                phase(Phase(LAST_ROUND, off, last=off == 3))

        last_use = LAST_ROUND * ROUND_USES + FIRST_USES + 3 + 3 + 2
        TAIL_USES = {name: last_use + n for n, name in enumerate([OT_LAST[0]] + [m for m, _ in MIX])}
        SETUP = {name: n for n, name in enumerate(SETUP_USES)}

        @block.sync
        def _(sp):
            def load_qk(slot):
                rows = slice(32 * slot, 32 * slot + 32)
                for i in range(PARTS):
                    for j in range(PARTS):
                        at = (PARTS * i + j) * H
                        sp.dma_start(qa[at:at + H, slot, :, :], q_parts[rows, i, :]).then_inc(qk_in[slot], 16)
                        sp.dma_start(ka[at:at + H, slot, :, :], k_parts[rows, j, :]).then_inc(qk_in[slot], 16)

            def load_rows(slot):
                for a in range(PARTS):
                    dst = qa[QK_ROWS + a:QK_ROWS + a + 1, slot, :, :].rearrange("a h (j s) -> a (h j) s", s=128)
                    sp.dma_start(dst, neg_parts[:, a, :]).then_inc(rows_in, 16)

            sp.sem_inc(out_done, 16)
            sp.dma_start(x_ln[:, :, :], x[0].rearrange("(p h) d -> p h d", h=T)).then_inc(x_in, 16)
            sp.dma_start(w_all[:, :, :], w_qkv.rearrange("n d e -> d n e")).then_inc(w_in, 16)
            sp.dma_start(wo[:, :], w_out.rearrange("n h d -> (n h) d")).then_inc(w_in, 16)
            for n, w in enumerate((w_r, w_k, w_v)):
                sp.dma_start(w_mix[:, n, :], w[:, :]).then_inc(w_in, 16)
            for n, m in enumerate((mu_r, mu_k)):
                sp.dma_start(mu[:, n:n + 1], m.rearrange("(d o) -> d o", o=1)).then_inc(w_in, 16)
            sp.wait_ge(zeroed, 3)
            sp.wait_ge(lo_ready, 4)
            load_qk(0)
            load_qk(1)
            sp.wait_ge(parts_ready, 1)
            load_rows(0)

            def phase(f):
                if f.project:
                    sp.wait_ge(xn_ready, f.per_round(2, 1))
                    nxt = x[bass.ds(f.i + 1, 1)]
                    sp.dma_start(x_ln[:, :, :], nxt.rearrange("b (p h) d -> p (b h) d", h=T)).then_inc(x_in, 16)
                if not (f.final and f.off >= 2):
                    slot = (f.off + 2) % GROUPS
                    if not f.first:
                        if f.off >= 2:
                            sp.wait_ge(s2_full, f.count(CHUNKS, -CHUNKS))
                        sp.wait_ge(lo_ready, f.per_round(4, 8 if f.off in (2, 3, 4) else 4))
                    load_qk(slot)
                if f.off == 3:
                    if f.final:
                        sp.wait_ge(y_ready, 2 * LAST_ROUND)
                        src = x[LAST_ROUND:LAST_ROUND + 1]
                    else:
                        src = x[bass.ds(f.i, 1)]
                    sp.dma_start(x1[:, :, :], src.rearrange("b (p h) d -> p (b h) d", h=T)).then_inc(x1_in, 16)
                if MAX_ROW[0] in f.uses:
                    sp.wait_ge(parts_ready, f.count(1, 2))
                    load_rows((f.off + 1) % GROUPS)
                if f.mix:
                    sp.wait_ge(y_ready, f.per_round(2, 2))
                    dst = out[bass.ds(f.i, 1)].rearrange("b (p h) d -> p (b h) d", h=T)
                    sp.dma_start(dst, y[:, :, :]).then_inc(out_done, 16)

            rounds(sp, phase)
            dst = out[LAST_ROUND].rearrange("(p h) d -> p h d", h=T)
            for u in range(2):
                sp.wait_ge(y_ready, 2 * LAST_ROUND + u + 1)
                sp.dma_start(dst[:, 4 * u:4 * u + 4, :], y[:, 4 * u:4 * u + 4, :]).then_inc(out_done, 16)
            sp.wait_ge(out_done, 16 * (B + 2))

        @block.gpsimd
        def _(pool):
            g = nc.gpsimd
            g.memset(ident[:, :], 0.0).then_inc(pool_setup, 1)
            g.memset(ident_bf[:, :], 0.0).then_inc(pool_setup, 1)
            g.memset(causal[:, :], 0.0).then_inc(pool_setup, 1)
            g.memset(minus_half[:, :], -0.5).then_inc(pool_setup, 1)
            g.memset(ones[:, :], 1.0).then_inc(consts_ready, 1)
            wait_apart(pool, pool_setup, 4)
            for m in (ident, ident_bf):
                g.affine_select(out=m[:, :], in_=m[:, :], compare_op=ALU.not_equal, fill=1.0, base=0,
                                pattern=[[-1, 128]], channel_multiplier=1).then_inc(consts_ready, 1)
            g.affine_select(out=causal[:, :], in_=causal[:, :], compare_op=ALU.is_ge, fill=LOW, base=0,
                            pattern=[[-1, 128]], channel_multiplier=1).then_inc(consts_ready, 1)

            def normalise(src, ln):
                wait_apart(pool, stats_ready, ln + 1)
                g.tensor_tensor(rstd[:, :], var_eps[:, :], minus_half[:, :], ALU.pow).then_inc(norm_step, 1)
                wait_apart(pool, norm_step, ln * 3 + 1)
                g.tensor_tensor(shift[:, :], mean_var[:, :, 0], rstd[:, :], ALU.mult).then_inc(norm_step, 1)
                wait_apart(pool, norm_step, ln * 3 + 2)
                g.tensor_scalar(shift[:, :], shift[:, :], -1.0, 1.0, ALU.mult, ALU.mult).then_inc(norm_step, 1)
                wait_apart(pool, norm_step, ln * 3 + 3)
                for h in range(T):
                    last = g.tensor_scalar(xn[:, h, :], src[:, h, :], rstd[:, h:h + 1], shift[:, h:h + 1],
                                           ALU.mult, ALU.add)
                last.then_inc(xn_ready, 1)

            def third_part(side, half, n):
                dst = (q_parts, k_parts)[side]
                cols = slice(HALF * half, HALF * half + HALF)
                wait_apart(pool, mid_ready, n + 1)
                g.tensor_tensor(dst[:, 2, cols], rest[:, half, :], dst[:, 1, cols], ALU.subtract).then_inc(lo_ready, 1)

            def place_values(slot):
                src = v_all[:, :, 32 * slot:32 * slot + 32].rearrange("p t (n h) -> p t n h", h=H)
                g.tensor_copy(va[:, slot, :, :, 0:H], src).then_inc(v_ready, 1)

            normalise(x_ln, 0)
            for n in range(4):
                third_part(n // 2, n % 2, n)
            wait_apart(pool, values_cleared, 1)
            wait_apart(pool, bank_read, SETUP["v1"] + 1)
            place_values(0)
            place_values(1)

            def scale_x(done):
                for side in range(2):
                    if side:
                        wait_apart(pool, mixed, done + 1)
                    g.tensor_scalar(scaled[:, :], xT[:, 1:1 + S], mu[:, side:side + 1], 1.0,
                                    ALU.mult, ALU.mult).then_inc(scaled_r, 1)

            def square_k(half, use):
                cols = slice(HALF * half, HALF * half + HALF)
                wait_apart(pool, bank_read, use + 1)
                g.tensor_tensor(k_act[:, cols], k_relu[:, cols], k_relu[:, cols], ALU.mult).then_inc(act_ready, 1)

            def phase(f):
                if not (f.final and f.off >= 2):
                    if f.off >= 2:
                        wait_apart(pool, sets_done, f.count(SETS, -SETS))
                    place_values((f.off + 2) % GROUPS)
                for step in range(CHUNKS):
                    if step in DIAGONAL:
                        wait_apart(pool, exp_done, f.count(CHUNKS, step + 1))
                        blocks = probs[:, step % PSLOTS, :].rearrange("p (a c) -> p a c", c=128)
                        blocks = blocks[:, 0:4:DIAGONAL[step], :] if DIAGONAL[step] else blocks[:, 0:1, :]
                        g.affine_select(out=blocks, in_=blocks, compare_op=ALU.is_ge, fill=0.0, base=0,
                                        pattern=[[0, blocks.shape[1]], [1, 128]],
                                        channel_multiplier=-1).then_inc(masked, 1)
                    name = f.steps.get(step)
                    if f.project:
                        if step == 9:
                            normalise(x_ln, f.per_round(2, 1))
                        if name and name.startswith("qk"):
                            n = int(name[2])
                            third_part(n // 2, n % 2, f.per_round(4, 4 + n))
                    if f.mix:
                        if step == 13:
                            normalise(x1, f.per_round(2, 2))
                        if name == "xT1":
                            wait_apart(pool, bank_read, f.use("xT1") + 1)
                            scale_x(f.per_round(2, 0))
                        if name in ("k0", "k1"):
                            square_k(int(name[1]), f.use(name))

            rounds(pool, phase)
            normalise(x1, 2 * LAST_ROUND + 1)
            wait_apart(pool, bank_read, TAIL_USES["xT1"] + 1)
            scale_x(2 * LAST_ROUND)
            for half in range(2):
                square_k(half, TAIL_USES[f"k{half}"])

        @block.scalar
        def _(act):
            def copy_out(dst, src, use):
                act.wait_ge(bank_full, use + 1)
                nc.scalar.activation(dst, src, ACT.Copy).then_inc(bank_read, 1)

            def transposed_x(u, use):
                dst = xT[:, 1:1 + S].rearrange("d (p h) -> d h p", h=T)[:, 4 * u:4 * u + 4, :]
                copy_out(dst, shared[:, :].rearrange("d (h p) -> d h p", h=4), use)

            def two_parts(n, use):
                dst = (q_parts, k_parts)[n // 2]
                cols = slice(HALF * (n % 2), HALF * (n % 2) + HALF)
                act.wait_ge(bank_full, use + 1)
                nc.scalar.activation(dst[:, 0, cols], shared[:, :], ACT.Copy).then_inc(hi_ready, 1)
                act.wait_ge(bank_read, use + 1)
                nc.scalar.activation(dst[:, 1, cols], rest[:, n % 2, :], ACT.Copy).then_inc(mid_ready, 1)

            def tanh_gate(half, use):
                cols = slice(HALF * half, HALF * half + HALF)
                act.wait_ge(bank_full, use + 1)
                nc.scalar.activation(gate[:, cols], shared[:, :], ACT.Tanh, scale=0.5).then_inc(bank_read, 1)

            def relu_k(half, use):
                cols = slice(HALF * half, HALF * half + HALF)
                act.wait_ge(bank_full, use + 1)
                nc.scalar.activation(k_relu[:, cols], shared[:, :], ACT.Relu).then_inc(bank_read, 1)

            copy_out(w_sum[:, :], shared[:, 0:D], SETUP["w_out"])
            copy_out(w_mixT[:, :, :].rearrange("p a b -> p (a b)"), shared[:, 0:3 * D], SETUP["w_t"])
            act.wait_ge(w_ready, 7)
            for u in range(2):
                transposed_x(u, SETUP[f"xT{u}"])
            for n in range(4):
                two_parts(n, SETUP[f"qk{n}"])
            for u in range(2):
                copy_out(v_all[:, 4 * u:4 * u + 4, :].rearrange("p a b -> p (a b)"), shared[:, :], SETUP[f"v{u}"])

            def read_acc(f, sets):
                act.wait_ge(sets_done, sets)
                nc.scalar.activation(oT[:, :], acc[:, :], ACT.Copy).then_inc(acc_read, 1)

            def phase(f):
                for step in range(CHUNKS):
                    act.wait_ge(s2_full, f.count(CHUNKS, step + 1))
                    if step >= PSLOTS:
                        act.wait_ge(sets_done, f.count(SETS, set_of(step - PSLOTS) + 1))
                    elif not f.first:
                        act.wait_ge(sets_done, f.count(SETS, set_of(step - PSLOTS + CHUNKS) + 1 - SETS))
                    nc.scalar.activation(probs[:, step % PSLOTS, :], bank2[step % RING][:, :], ACT.Exp,
                                         scale=SCALE).then_inc(exp_done, 1)
                    if step == 2 and not f.first:
                        read_acc(f, f.count(SETS, 0))
                    if step == SET_ENDS[HALF_SETS - 1] + LAG:
                        if not f.first:
                            act.wait_ge(bank_full, f.use(OT_LAST[0]) + 1)
                        read_acc(f, f.count(SETS, HALF_SETS))
                    name = f.steps.get(step)
                    if name in ("xT0", "xT1"):
                        transposed_x(int(name[2]), f.use(name))
                    elif f.project and name and name.startswith("qk"):
                        n = int(name[2])
                        if n == 0:
                            act.wait_ge(qk_in[(f.off + 2) % GROUPS], f.fills(2))
                        two_parts(n, f.use(name))
                    elif f.project and name in ("v0", "v1"):
                        u = int(name[1])
                        if u == 0:
                            act.wait_ge(v_ready, f.count(1, 3))
                        copy_out(v_all[:, 4 * u:4 * u + 4, :].rearrange("p a b -> p (a b)"), shared[:, :], f.use(name))
                    elif name in ("r0", "r1"):
                        tanh_gate(int(name[1]), f.use(name))
                    elif name in ("k0", "k1"):
                        relu_k(int(name[1]), f.use(name))

            rounds(act, phase)
            read_acc(None, SETS * B * GROUPS)
            for u in range(2):
                transposed_x(u, TAIL_USES[f"xT{u}"])
            for half in range(2):
                tanh_gate(half, TAIL_USES[f"r{half}"])
            for half in range(2):
                relu_k(half, TAIL_USES[f"k{half}"])

        @block.vector
        def _(dve):
            v = nc.vector

            def reduce_chunk(r, bank, done, first_ever):
                piece = PASS1[r][0]
                h, j = piece[0], piece[1]
                src = bank[:, :]
                if r < 16:
                    dst = far_max[:, h, j - 4:j - 3]
                elif r < 24:
                    dst = part_max[:, h, j, 0:1]
                elif r < 32:
                    dst = part_max[:, h, :, :].rearrange("p t c -> p (t c)")[:, 3 * j + 2:3 * j + 6]
                    src = src.rearrange("p (a c) -> p a c", c=128)
                else:
                    dst = part_max[:, h:h + 2, j + 1, 0]
                    src = src.rearrange("p (a c) -> p a c", c=256)
                dve.wait_ge(s1_full, done + 1)
                v.reduce_max(dst, src, AX.X).then_inc(s1_read, 1)

            def finish_max(groups, chunks):
                dve.wait_ge(s1_read, chunks)
                v.reduce_max(q_max[:, :].rearrange("p (g b a) -> p g a b", b=2, a=2),
                             part_max[:, :, :, :].rearrange("p h (c a b) k -> p (h c) a b k", a=2, b=2),
                             AX.X).then_inc(far_done, 1)
                dve.wait_ge(far_done, groups + 1)
                far = q_max[:, :].rearrange("p (h t) -> p h t", t=T)[:, :, 4:8]
                v.tensor_tensor(far, far, far_max[:, :, :], ALU.max).then_inc(max_ready, 1)
                dve.wait_ge(max_ready, groups + 1)

            def split_max(use, rows, steps):
                got = shared[0:GH * T, 0:128]
                dve.wait_ge(bank_full, use + 1)
                if rows is not None:
                    dve.wait_ge(rows_in, rows)
                v.tensor_scalar(neg_parts[:, 0, :], got, -1.0, None, ALU.mult).then_inc(split_step, 1)
                dve.wait_ge(split_step, steps + 1)
                v.scalar_tensor_tensor(neg_rest[:, :], got, -1.0, neg_parts[:, 0, :], ALU.mult,
                                       ALU.subtract).then_inc(bank_read, 1)
                dve.wait_ge(bank_read, use + 1)
                v.tensor_copy(neg_parts[:, 1, :], neg_rest[:, :]).then_inc(split_step, 1)
                dve.wait_ge(split_step, steps + 2)
                v.tensor_tensor(neg_parts[:, 2, :], neg_rest[:, :], neg_parts[:, 1, :], ALU.subtract).then_inc(parts_ready, 1)

            def bn(src, tiles):
                for h in tiles:
                    v.bn_stats(stats[:, h, :], src[:, h, :]).then_inc(bn_done, 1)

            def bn_end(ln):
                wait_apart(dve, bn_done, ln * (2 * T) + T)
                for h in range(T):
                    v.bn_aggr(mean_var[:, h, :], stats[:, h, :]).then_inc(bn_done, 1)
                wait_apart(dve, bn_done, ln * (2 * T) + 2 * T)
                v.tensor_scalar(var_eps[:, :], mean_var[:, :, 1], EPS, None, ALU.add).then_inc(stats_ready, 1)

            def rest_of(n, use):
                cols = slice(HALF * (n % 2), HALF * (n % 2) + HALF)
                dst = (q_parts, k_parts)[n // 2]
                v.tensor_tensor(rest[:, n % 2, :], shared[:, :], dst[:, 0, cols], ALU.subtract).then_inc(bank_read, 1)

            def normalise_out(slot, half, use, units):
                got = shared[:, :].rearrange("p (j n c) -> p j n c", j=4, n=GH)
                dve.wait_ge(bank_full, use + 1)
                v.reciprocal(inv[:, :, :], got[:, :, :, H]).then_inc(inv_step, 1)
                dve.wait_ge(inv_step, units * 2 + 1)
                w = w_sum[:, :].rearrange("p (n j) -> p j n", j=T)[:, 4 * half:4 * half + 4, GH * slot:GH * slot + GH]
                v.tensor_tensor(inv_w[:, :, :], inv[:, :, :], w, ALU.mult).then_inc(inv_step, 1)
                dve.wait_ge(inv_step, units * 2 + 2)
                dst = att[:, :, :].rearrange("p h (n j) -> p j n h", j=T)[:, 4 * half:4 * half + 4, GH * slot:GH * slot + GH, :]
                v.tensor_tensor(dst, got[:, :, :, 0:H], inv_w[:, :, :].unsqueeze(3).broadcast_to([128, 4, GH, H]),
                                ALU.mult).then_inc(bank_read, 1)

            def add_attention(batches, use):
                dve.wait_ge(x1_in, batches * 16 + 16)
                dve.wait_ge(bank_read, use + 1)
                v.tensor_tensor(x1[:, :, :], att[:, :, :], x1[:, :, :], ALU.add).then_inc(att_ready, 1)
                dve.wait_ge(att_ready, batches + 1)

            def mix_x(side, n):
                dve.wait_ge(scaled_r, n + 1)
                v.scalar_tensor_tensor((xr, xk)[side][:, :], xT[:, 0:S], one_less_mu[:, side:side + 1],
                                       scaled[:, :], ALU.mult, ALU.add).then_inc(mixed, 1)

            def gate_end(batches, use):
                dve.wait_ge(bank_read, use + 1)
                v.tensor_scalar(gate[:, :], gate[:, :], 0.5, 0.5, ALU.mult, ALU.add).then_inc(gate_ready, 1)
                dve.wait_ge(gate_ready, batches + 1)

            def gate_v(half, use):
                cols = slice(HALF * half, HALF * half + HALF)
                dve.wait_ge(bank_full, use + 1)
                v.tensor_tensor(yT[:, cols], shared[:, :], gate[:, cols], ALU.mult).then_inc(bank_read, 1)

            def add_y(u, use, stored):
                dve.wait_ge(bank_full, use + 1)
                if u == 0:
                    dve.wait_ge(out_done, stored)
                v.tensor_tensor(y[:, 4 * u:4 * u + 4, :], shared[:, :].rearrange("p (h d) -> p h d", h=4),
                                x1[:, 4 * u:4 * u + 4, :], ALU.add).then_inc(bank_read, 1)

            v.memset(va[:, :, :, :, :], 0.0).then_inc(w_ready, 1)
            v.memset(part_max[:, :, :, :], 3 * LOW).then_inc(w_ready, 1)
            v.memset(xT[:, 0:1], 0.0).then_inc(w_ready, 1)
            dve.wait_ge(w_ready, 1)
            v.memset(va[:, :, :, :, H:H + 1], 1.0).then_inc(values_cleared, 1)
            dve.wait_ge(x_in, 16)
            bn(x_ln, range(T))
            bn_end(0)
            dve.wait_ge(w_in, 7 * 16)
            qkv = w_all[:, :, :].rearrange("p (g n) e -> p g e n", n=GH)
            v.tensor_copy(wq[:, :].rearrange("p (g e n) -> p g e n", e=H, n=GH), qkv[:, :, 0:H, :]).then_inc(w_ready, 1)
            v.tensor_copy(wk[:, :].rearrange("p (g e n) -> p g e n", e=H, n=GH), qkv[:, :, H:2 * H, :]).then_inc(w_ready, 1)
            v.tensor_copy(wv[:, :].rearrange("p (n h) -> p n h", h=H), w_all[:, :, 2 * H:3 * H]).then_inc(w_ready, 1)
            v.tensor_scalar(one_less_mu[:, :], mu[:, :], -1.0, 1.0, ALU.mult, ALU.add).then_inc(w_ready, 1)
            v.memset(qa[64:96, :, :, :].bitcast(F32), 0.0).then_inc(zeroed, 1)
            v.memset(ka[64:96, :, :, :].bitcast(F32), 0.0).then_inc(zeroed, 1)
            v.memset(ka[96:96 + PARTS, :, :, :], 1.0).then_inc(zeroed, 1)
            for n in range(4):
                dve.wait_ge(hi_ready, n + 1)
                if n >= 2:
                    dve.wait_ge(lo_ready, n - 1)
                rest_of(n, SETUP[f"qk{n}"])
            for n in range(CHUNKS + AHEAD):
                reduce_chunk(n % CHUNKS, bank1[n % RING], n, True)
                if n == CHUNKS - 1:
                    finish_max(0, CHUNKS)
                if n == CHUNKS + 2:
                    split_max(SETUP["max"], None, 0)

            def phase(f):
                for step in range(CHUNKS):
                    ahead = f.first_pass(step)
                    if ahead:
                        groups, slot, r = ahead
                        reduce_chunk(r, bank1[r % RING], f.count(CHUNKS, groups * CHUNKS + r), False)
                        if r == CHUNKS - 1:
                            finish_max(f.count(1, groups), f.count(CHUNKS, (groups + 1) * CHUNKS))
                    name = f.steps.get(step)
                    if name == OT_LAST[0]:
                        normalise_out((f.off - 1) % GROUPS, 1, f.use(name), f.count(2, -1))
                    elif name == OT_FIRST[0]:
                        normalise_out(f.slot, 0, f.use(name), f.count(2, 0))
                    elif name == MAX_ROW[0]:
                        split_max(f.use(name), f.count(48, 48), f.count(2, 2))
                    elif f.project and name and name.startswith("qk"):
                        n = int(name[2])
                        dve.wait_ge(hi_ready, f.per_round(4, 4 + n + 1))
                        dve.wait_ge(lo_ready, f.per_round(4, 4 + n - 1))
                        rest_of(n, f.use(name))
                    elif f.mix and name in ("v0", "v1"):
                        gate_v(int(name[1]), f.use(name))
                    elif f.mix and name in ("y0", "y1"):
                        add_y(int(name[1]), f.use(name), f.per_round(16, 16))
                        v_done(f.use(name) + 1)
                    if f.project and 4 <= step < 8:
                        if step == 4:
                            dve.wait_ge(x_in, f.per_round(16, 32))
                        bn(x_ln, (2 * (step - 4), 2 * (step - 4) + 1))
                        if step == 7:
                            bn_end(f.per_round(2, 1))
                    if f.mix:
                        if step == 7:
                            add_attention(f.per_round(1, 0), f.use(OT_LAST[0]))
                        if 8 <= step < 12:
                            bn(x1, (2 * (step - 8), 2 * (step - 8) + 1))
                        if step == 11:
                            bn_end(f.per_round(2, 2))
                        if name == "xT1" or step == 24:
                            side = int(step == 24)
                            mix_x(side, f.per_round(2, side))
                        if name == "k1":
                            gate_end(f.per_round(1, 0), f.use("r1"))

            def v_done(use):
                dve.wait_ge(bank_read, use)
                dve.sem_inc(y_ready, 1)

            rounds(dve, phase)
            normalise_out(GROUPS - 1, 1, TAIL_USES[OT_LAST[0]], 2 * B * GROUPS - 1)
            add_attention(LAST_ROUND, TAIL_USES[OT_LAST[0]])
            bn(x1, range(T))
            bn_end(2 * LAST_ROUND + 1)
            for side in range(2):
                mix_x(side, 2 * LAST_ROUND + side)
            gate_end(LAST_ROUND, TAIL_USES["r1"])
            for half in range(2):
                gate_v(half, TAIL_USES[f"v{half}"])
            for u in range(2):
                add_y(u, TAIL_USES[f"y{u}"], 16 * B)
                v_done(TAIL_USES[f"y{u}"] + 1)

        @block.tensor
        def _(pe):
            mm = nc.tensor.matmul

            def take_bank(use):
                pe.wait_ge(bank_read, use)

            def first_pass(slot, r, bank, done):
                if not (isinstance(done, int) and done < RING):
                    pe.wait_ge(s1_read, done + (1 - RING))
                for h, j, k0, n, at, diag in PASS1[r]:
                    last = mm(bank[:, at:at + n], qa[0:QK_ROWS, slot, h, 128 * j:128 * j + 128],
                              ka[0:QK_ROWS, slot, h, k0:k0 + n], start=True, stop=diag is None)
                    if diag is not None:
                        last = mm(bank[:, diag:diag + 128], ident_bf[:, :], causal[:, :], start=False, stop=True)
                last.then_inc(s1_full, 1)

            def second_pass(slot, c, bank):
                for h, i, q0, n, at in PASS2[c]:
                    last = mm(bank[:, at:at + n], ka[0:ALL_ROWS, slot, h, 128 * i:128 * i + 128],
                              qa[0:ALL_ROWS, slot, h, q0:q0 + n], start=True, stop=True)
                last.then_inc(s2_full, 1)

            def values(slot, k):
                pieces = pieces_of_set(k)
                for i, q0, n, heads in pieces:
                    at = q0 % HALF
                    for h, c, place in heads:
                        last = mm(acc[VW * h:VW * h + VW, at:at + n], va[:, slot, i, h, :],
                                  probs[:, c % PSLOTS, place:place + n], start=i == 0,
                                  stop=k in (HALF_SETS - 1, SETS - 1))
                last.then_inc(sets_done, 1)

            def transpose_out(use):
                take_bank(use)
                for j in range(4):
                    last = nc.tensor.transpose(shared[:, 128 * j:128 * j + 128], oT[:, 128 * j:128 * j + 128], ident[:, :])
                last.then_inc(bank_full, 1)

            def transpose_max(use):
                take_bank(use)
                nc.tensor.transpose(shared[0:GH * T, 0:128], q_max[:, :], ident[:, :]).then_inc(bank_full, 1)

            def transpose_x(u, use):
                take_bank(use)
                for h in range(4):
                    last = nc.tensor.transpose(shared[:, 128 * h:128 * h + 128], xn[:, 4 * u + h, :], ident[:, :])
                last.then_inc(bank_full, 1)

            def project_qk(n, use):
                take_bank(use)
                half = n % 2
                mm(shared[:, :], (wq, wk)[n // 2][:, :], xT[:, 1 + HALF * half:1 + HALF * half + HALF],
                   start=True, stop=True).then_inc(bank_full, 1)

            def project_v(u, use):
                take_bank(use)
                for t in range(4):
                    at = 1 + 128 * (4 * u + t)
                    last = mm(shared[:, 128 * t:128 * t + 128], xT[:, at:at + 128], wv[:, :], start=True, stop=True)
                last.then_inc(bank_full, 1)

            def mix_product(n, src, half, use):
                take_bank(use)
                mm(shared[:, :], w_mixT[:, n, :], src[:, HALF * half:HALF * half + HALF],
                   start=True, stop=True).then_inc(bank_full, 1)

            def transpose_y(u, use):
                take_bank(use)
                tiles = yT[:, :].rearrange("d (p h) -> d h p", h=T)
                for h in range(4):
                    last = nc.tensor.transpose(shared[:, 128 * h:128 * h + 128], tiles[:, 4 * u + h, :], ident[:, :])
                last.then_inc(bank_full, 1)

            pe.wait_ge(consts_ready, 4)
            pe.wait_ge(w_in, 7 * 16)
            mm(shared[:, 0:D], ones[:, :], wo[:, :], start=True, stop=True).then_inc(bank_full, 1)
            take_bank(SETUP["w_t"])
            for n in range(3):
                last = nc.tensor.transpose(shared[:, 128 * n:128 * n + 128], w_mix[:, n, :], ident[:, :])
            last.then_inc(bank_full, 1)
            pe.wait_ge(xn_ready, 1)
            for u in range(2):
                transpose_x(u, SETUP[f"xT{u}"])
            pe.wait_ge(w_ready, 7)
            for n in range(4):
                project_qk(n, SETUP[f"qk{n}"])
            for u in range(2):
                project_v(u, SETUP[f"v{u}"])
            for n in range(CHUNKS + AHEAD):
                if n % CHUNKS == 0:
                    pe.wait_ge(qk_in[n // CHUNKS], 16 * QK_DMAS)
                first_pass(n // CHUNKS, n % CHUNKS, bank1[n % RING], n)
                if n == CHUNKS + 2:
                    pe.wait_ge(max_ready, 1)
                    transpose_max(SETUP["max"])

            def phase(f):
                for step in range(CHUNKS):
                    if step == 0:
                        pe.wait_ge(rows_in, f.count(48, 48))
                    if step >= RING or not f.first:
                        pe.wait_ge(exp_done, f.count(CHUNKS, step + 1 - RING))
                    second_pass(f.slot, step, bank2[step % RING])
                    ahead = f.first_pass(step)
                    if ahead:
                        groups, slot, r = ahead
                        if r == 0:
                            pe.wait_ge(qk_in[slot], f.fills(groups))
                        first_pass(slot, r, bank1[r % RING], f.count(CHUNKS, groups * CHUNKS + r))
                    if step - LAG in SET_ENDS:
                        k = SET_ENDS.index(step - LAG)
                        end = SET_ENDS[k]
                        pe.wait_ge(exp_done, f.count(CHUNKS, end + 1))
                        if end in DIAGONAL:
                            pe.wait_ge(masked, f.count(MASKS, masks_until(end)))
                        if k == 0:
                            pe.wait_ge(v_ready, f.count(1, 1))
                        if k in (0, HALF_SETS) and not (f.first and k == 0):
                            pe.wait_ge(acc_read, f.count(2, int(k > 0)))
                        values(f.slot, k)
                    elif step - LAG + CHUNKS in SET_ENDS and not f.first:
                        k = SET_ENDS.index(step - LAG + CHUNKS)
                        end = SET_ENDS[k]
                        pe.wait_ge(exp_done, f.count(CHUNKS, end + 1 - CHUNKS))
                        pe.wait_ge(masked, f.count(MASKS, masks_until(end) - MASKS))
                        values((f.off - 1) % GROUPS, k)
                    name = f.steps.get(step)
                    if not name:
                        continue
                    use = f.use(name)
                    if name == OT_LAST[0]:
                        pe.wait_ge(acc_read, f.count(2, 0))
                        transpose_out(use)
                    elif name == OT_FIRST[0]:
                        pe.wait_ge(acc_read, f.count(2, 1))
                        transpose_out(use)
                    elif name == MAX_ROW[0]:
                        pe.wait_ge(max_ready, f.count(1, 2))
                        transpose_max(use)
                    elif name in ("xT0", "xT1"):
                        pe.wait_ge(xn_ready, f.per_round(2, 2 if f.project else 3))
                        transpose_x(int(name[2]), use)
                    elif name.startswith("qk"):
                        project_qk(int(name[2]), use)
                    elif f.project:
                        project_v(int(name[1]), use)
                    elif name in ("r0", "r1"):
                        pe.wait_ge(mixed, f.per_round(2, 1))
                        mix_product(0, xr, int(name[1]), use)
                    elif name in ("k0", "k1"):
                        pe.wait_ge(mixed, f.per_round(2, 2))
                        mix_product(1, xk, int(name[1]), use)
                    elif name in ("v0", "v1"):
                        pe.wait_ge(act_ready, f.per_round(2, int(name[1]) + 1))
                        mix_product(2, k_act, int(name[1]), use)
                    else:
                        transpose_y(int(name[1]), use)

            rounds(pe, phase)
            for k in (SETS - 2, SETS - 1):
                pe.wait_ge(exp_done, CHUNKS * (B * GROUPS - 1) + SET_ENDS[k] + 1)
                pe.wait_ge(masked, MASKS * (B * GROUPS - 1) + masks_until(SET_ENDS[k]))
                values(GROUPS - 1, k)
            pe.wait_ge(acc_read, 2 * B * GROUPS)
            transpose_out(TAIL_USES[OT_LAST[0]])
            pe.wait_ge(xn_ready, 2 * B)
            for u in range(2):
                transpose_x(u, TAIL_USES[f"xT{u}"])
            pe.wait_ge(mixed, 2 * LAST_ROUND + 1)
            for half in range(2):
                mix_product(0, xr, half, TAIL_USES[f"r{half}"])
            pe.wait_ge(mixed, 2 * LAST_ROUND + 2)
            for half in range(2):
                mix_product(1, xk, half, TAIL_USES[f"k{half}"])
            for half in range(2):
                pe.wait_ge(act_ready, 2 * LAST_ROUND + half + 1)
                mix_product(2, k_act, half, TAIL_USES[f"v{half}"])
            for u in range(2):
                transpose_y(u, TAIL_USES[f"y{u}"])


def kernel(**inputs):
    import numpy as np
    import concourse.bacc as bacc
    from concourse.bass_utils import run_bass_kernel_spmd

    names = ["L0_attn_x", "L0_attn_W_qkv", "L0_attn_W_out", "L0_ffn_W_r", "L0_ffn_W_k", "L0_ffn_W_v",
             "L0_ffn_mu_r", "L0_ffn_mu_k"]
    nc = bacc.Bacc("TRN2", target_bir_lowering=False, num_devices=1)
    arrays, args = {}, []
    for name in names:
        a = np.ascontiguousarray(inputs[name])
        arrays[f"in_{name}"] = a
        args.append(nc.dram_tensor(f"in_{name}", a.shape, mybir.dt.from_np(a.dtype), kind="ExternalInput").ap())
    args.append(nc.dram_tensor("out_x", (B, S, D), F32, kind="ExternalOutput").ap())
    build(nc, *args)
    r = run_bass_kernel_spmd(nc, [arrays], core_ids=[0])
    return r.results[0]["out_x"]
```

```python
import concourse.bass as bass
import concourse.mybir as mybir
from contextlib import ExitStack

F32 = mybir.dt.float32
BF16 = mybir.dt.bfloat16
ALU = mybir.AluOpType
ACT = mybir.ActivationFunctionType
AX = mybir.AxisListType

B, S, D, N, H = 4, 1024, 128, 16, 8
T = S // 128
GH = 4
GROUPS = N // GH
HALF = S // 2
PARTS = 3
QK_ROWS = 96
ALL_ROWS = QK_ROWS + PARTS
VW = 32
CHUNKS = 36
AHEAD = 12
LAG = 3
RING = 3
PSLOTS = 12
SCALE = H ** -0.5
EPS = 1e-5
LOW = -1e30
QK_DMAS = 2 * PARTS * PARTS

def _pass2():
    chunks = []
    for half in range(2):
        base, t0 = half * HALF, half * 4
        for i in range(t0):
            chunks += [[(h, i, base, 512, 0)] for h in range(GH)]
        chunks += [[(h, t0, base, 512, 0)] for h in range(GH)]
        chunks += [[(h, t0 + 1, base + 128, 384, 0), (h, t0 + 3, base + 384, 128, 384)] for h in range(GH)]
        chunks += [[(h, t0 + 2, base + 256, 256, 256 * (h % 2)) for h in (p, p + 1)] for p in (0, 2)]
    return chunks


PASS2 = _pass2()
SET_ENDS = [3, 7, 9, 13, 17, 21, 25, 29, 33, 35]
SETS = len(SET_ENDS)
HALF_SETS = 3
DIAGONAL = {c: 0 for c in (0, 1, 2, 3, 26, 27, 28, 29)}
DIAGONAL |= {c: 3 for c in (4, 5, 6, 7, 30, 31, 32, 33)}
DIAGONAL |= {c: 2 for c in (8, 9, 34, 35)}
MASKS = len(DIAGONAL)
JOINED = D - D // GROUPS


def masks_until(c):
    return sum(x <= c for x in DIAGONAL)


def set_of(c):
    return next(k for k, e in enumerate(SET_ENDS) if e >= c)


def pieces_of_set(k):
    first = SET_ENDS[k - 1] + 1 if k else 0
    found = {}
    for c in range(first, SET_ENDS[k] + 1):
        for h, i, q0, n, at in PASS2[c]:
            found.setdefault((i, q0, n), []).append((h, c, at))
    return [(i, q0, n, hs) for (i, q0, n), hs in found.items()]


def _pass1():
    chunks = [[(h, j, 0, 512, 0, None)] for j in range(4, 8) for h in range(GH)]
    chunks += [[(h, 3, 0, 512, 0, 384)] for h in range(GH)]
    chunks += [[(h, 7, 512, 512, 0, 384)] for h in range(GH)]
    for t0 in (0, 4):
        k0 = 128 * t0
        chunks += [[(h, t0, k0, 128, 0, 0), (h, t0 + 2, k0, 384, 128, 384)] for h in range(GH)]
    for t0 in (0, 4):
        k0 = 128 * t0
        chunks += [[(h, t0 + 1, k0, 256, 256 * (h % 2), 256 * (h % 2) + 128) for h in (p, p + 1)] for p in (0, 2)]
    return chunks


PASS1 = _pass1()

OT_LAST, OT_FIRST, MAX_ROW = ("out, 2nd half of the group before", 5), ("out, 1st half", 15), ("max", 26)
PROJECT = {1: [("xT0", 24), ("xT1", 27), ("qk0", 30), ("qk1", 33)],
           2: [("qk2", 2), ("qk3", 8), ("v0", 11), ("v1", 13)]}
MIX = [("xT0", 17), ("xT1", 18), ("r0", 21), ("r1", 23), ("k0", 24), ("k1", 28), ("v0", 30), ("v1", 32), ("y0", 34), ("y1", 35)]


def uses_of(off, project, mix, first=False, last=False):
    uses = [] if first else [OT_LAST]
    uses += [OT_FIRST] + ([] if last else [MAX_ROW]) + PROJECT.get(project, []) + (MIX if mix else [])
    uses.sort(key=lambda u: u[1])
    return {name: (n, step) for n, (name, step) in enumerate(uses)}


FIRST_USES = 1 + 2
ROUND_USES = 7 + 7 + 3 + 13
USES_BEFORE = {0: -2, 1: 0, 2: 7, 3: 14, 4: 17}


class Phase:

    def __init__(self, i, off, project=0, mix=False, first=False, last=False, eng=None, products=None):
        self.i, self.off, self.project, self.mix = i, off, project, mix
        self.eng, self.products = eng, products
        self.first, self.last = first, last
        self.final = isinstance(i, int) and i == LAST_ROUND
        self.slot = off % GROUPS
        self.uses = uses_of(off, project, mix, first, last)
        self.steps = {step: name for name, (_, step) in self.uses.items()}
        self.before = {1: 0, 2: 3, 3: 6}[off] if self.final else USES_BEFORE[off]

    def per_round(self, each, more):
        if isinstance(self.i, int):
            return self.i * each + more
        if each not in self.products:
            self.products[each] = self.eng.snap(self.i * each)
        return self.products[each] + more

    def count(self, per_group, more):
        return self.per_round(GROUPS * per_group, self.off * per_group + more)

    def fills(self, ahead):
        return self.per_round(16 * QK_DMAS, 16 * QK_DMAS * ((self.off + ahead) // GROUPS + 1))

    def use(self, name):
        return self.per_round(ROUND_USES, FIRST_USES + self.before + self.uses[name][0])

    def first_pass(self, step):
        n = step + AHEAD
        ahead, r = 1 + n // CHUNKS, n % CHUNKS
        if self.last or (self.final and self.off + ahead >= GROUPS):
            return None
        return ahead, (self.off + ahead) % GROUPS, r


LAST_ROUND = B - 1


def build(nc, x, w_qkv, w_out, w_r, w_k, w_v, mu_r, mu_k, out):
    nc.disable_value_cache = True
    ctx = ExitStack()
    with ctx:
        def sb(name, shape, dt=F32):
            return ctx.enter_context(nc.sbuf_tensor(name, shape, dt))

        def ps(name):
            return ctx.enter_context(nc.psum_tensor(name, [128, 512], F32))

        def sem(name):
            return ctx.enter_context(nc.semaphore(name))

        qa = sb("qa", [128, GROUPS, GH, S], BF16)
        ka = sb("ka", [128, GROUPS, GH, S], BF16)
        va = sb("va", [128, GROUPS, T, GH, VW])
        probs = sb("probs", [128, PSLOTS, 512])
        q_parts = sb("q_parts", [128, PARTS, S], BF16)
        k_parts = sb("k_parts", [128, PARTS, S], BF16)
        v_all = sb("v_all", [128, T, D])
        x_ln = sb("x_ln", [128, T, D])
        x1 = sb("x1", [128, T, D])
        att = sb("att", [128, T, D])
        xn = sb("xn", [128, T, D])
        xT = sb("xT", [128, 1 + S])
        scaled = sb("scaled", [128, S])
        xr = sb("xr", [128, S])
        xk = sb("xk", [128, S])
        gate = sb("gate", [128, S])
        k_relu = sb("k_relu", [128, S])
        k_act = sb("k_act", [128, S])
        yT = sb("yT", [128, S])
        y = sb("y", [128, T, D])
        fill = sb("fill", [128, 2])
        rest = sb("rest", [128, 2, 512])
        oT = sb("oT", [128, 512])
        inv = sb("inv", [128, 4, GH])
        inv_w = sb("inv_w", [128, 4, GH])
        part_max = sb("part_max", [128, GH, T, 3])
        far_max = sb("far_max", [128, GH, 4])
        q_max = sb("q_max", [128, GH * T])
        neg_rest = sb("neg_rest", [GH * T, 128])
        neg_parts = sb("neg_parts", [GH * T, PARTS, 128], BF16)
        stats = sb("stats", [128, T, 6])
        mean_var = sb("mean_var", [128, T, 2])
        var_eps = sb("var_eps", [128, T])
        rstd = sb("rstd", [128, T])
        shift = sb("shift", [128, T])
        minus_half = sb("minus_half", [128, T])
        w_all = sb("w_all", [128, N, 3 * H])
        wq = sb("wq", [128, D])
        wk = sb("wk", [128, D])
        wv = sb("wv", [128, D])
        wo = sb("wo", [128, D])
        w_sum = sb("w_sum", [128, D])
        w_mix = sb("w_mix", [128, 3, D])
        w_mixT = sb("w_mixT", [128, 3, D])
        mu = sb("mu", [128, 2])
        one_less_mu = sb("one_less_mu", [128, 2])
        ident = sb("ident", [128, 128])
        ident_bf = sb("ident_bf", [128, 128], BF16)
        causal = sb("causal", [128, 128], BF16)
        ones = sb("ones", [128, 128])

        bank2 = [ps(f"scores2_{n}") for n in range(RING)]
        bank1 = [ps(f"scores1_{n}") for n in range(RING)]
        acc = ps("acc")
        shared = ps("shared")

        x_in = sem("x_in")
        w_in = sem("w_in")
        x1_in = sem("x1_in")
        qk_in = [sem(f"qk_in{n}") for n in range(GROUPS)]
        rows_in = sem("rows_in")
        out_done = sem("out_done")
        pool_setup = sem("pool_setup")
        consts_ready = sem("consts_ready")
        fill_ready = sem("fill_ready")
        zeroed = sem("zeroed")
        column_ready = sem("column_ready")
        w_ready = sem("w_ready")
        setup_full = sem("setup_full")
        setup_copied = sem("setup_copied")
        rest_done = sem("rest_done")
        tail_full = sem("tail_full")
        tail_done = sem("tail_done")
        rstd_ready = sem("rstd_ready")
        shift_ready = sem("shift_ready")
        bn_done = sem("bn_done")
        stats_ready = sem("stats_ready")
        xn_ready = sem("xn_ready")
        bank_full = sem("bank_full")
        bank_read = sem("bank_read")
        hi_ready = sem("hi_ready")
        mid_ready = sem("mid_ready")
        lo_ready = sem("lo_ready")
        v_ready = sem("v_ready")
        s1_full = sem("s1_full")
        s1_read = sem("s1_read")
        far_done = sem("far_done")
        max_ready = sem("max_ready")
        split_step = sem("split_step")
        parts_ready = sem("parts_ready")
        s2_full = sem("s2_full")
        exp_done = sem("exp_done")
        masked = sem("masked")
        sets_done = sem("sets_done")
        acc_read = sem("acc_read")
        inv_step = sem("inv_step")
        joined = sem("joined")
        att_ready = sem("att_ready")
        scaled_r = sem("scaled_r")
        scaled_k = sem("scaled_k")
        mixed = sem("mixed")
        gate_ready = sem("gate_ready")
        yT_ready = sem("yT_ready")
        act_ready = sem("act_ready")
        y_ready = sem("y_ready")

        values_cleared = sem("values_cleared")
        pool_passed = sem("pool_passed")
        dve_passed = sem("dve_passed")

        block = ctx.enter_context(nc.Block())

        def wait_apart(eng, sem, value):
            eng.wait_ge(sem, value)
            if not isinstance(value, int):
                eng.sem_inc(pool_passed if eng is nc.gpsimd else dve_passed, 1)

        def rounds(eng, phase):
            phase(Phase(0, 0, first=True))
            with eng.Fori(0, B - 1) as i:
                multiples = {}
                phase(Phase(i, 1, project=1, eng=eng, products=multiples))
                phase(Phase(i, 2, project=2, eng=eng, products=multiples))
                phase(Phase(i, 3, eng=eng, products=multiples))
                phase(Phase(i, 4, mix=True, eng=eng, products=multiples))
            for off in (1, 2, 3):
                phase(Phase(LAST_ROUND, off, last=off == 3))

        tail_use = LAST_ROUND * ROUND_USES + FIRST_USES + 3 + 3 + 2
        halves = (slice(0, HALF), slice(HALF, S))
        qk_banks = bank1 + [shared]

        @block.sync
        def _(sp):
            def load_part(slot, side, n):
                rows = slice(32 * slot, 32 * slot + 32)
                for m in range(PARTS):
                    at = H * (PARTS * m + n if side else PARTS * n + m)
                    sp.dma_start((qa, ka)[side][at:at + H, slot, :, :],
                                 (q_parts, k_parts)[side][rows, n, :]).then_inc(qk_in[slot], 16)

            def load_qk(slot):
                for side in range(2):
                    for n in range(PARTS):
                        load_part(slot, side, n)

            def load_rows(slot):
                for a in range(PARTS):
                    dst = qa[QK_ROWS + a:QK_ROWS + a + 1, slot, :, :].rearrange("a h (j s) -> a (h j) s", s=128)
                    sp.dma_start(dst, neg_parts[:, a, :]).then_inc(rows_in, 16)

            sp.sem_inc(out_done, 16)
            sp.dma_start(x_ln[:, :, :], x[0].rearrange("(p h) d -> p h d", h=T)).then_inc(x_in, 16)
            sp.dma_start(w_all[:, :, :], w_qkv.rearrange("n d e -> d n e")).then_inc(w_in, 16)
            sp.dma_start(wo[:, :], w_out.rearrange("n h d -> (n h) d")).then_inc(w_in, 16)
            for n, w in enumerate((w_r, w_k, w_v)):
                sp.dma_start(w_mix[:, n, :], w[:, :]).then_inc(w_in, 16)
            for n, m in enumerate((mu_r, mu_k)):
                sp.dma_start(mu[:, n:n + 1], m.rearrange("(d o) -> d o", o=1)).then_inc(w_in, 16)
            sp.wait_ge(zeroed, 1)
            for side in range(2):
                for n, part_ready in enumerate((hi_ready, mid_ready, lo_ready)):
                    sp.wait_ge(part_ready, 2 * side + 2)
                    load_part(0, side, n)
            sp.wait_ge(zeroed, 2)
            load_qk(1)
            sp.wait_ge(parts_ready, 1)
            load_rows(0)

            def phase(f):
                if f.project == 1:
                    sp.wait_ge(xn_ready, f.per_round(4, 2))
                    nxt = x[bass.ds(f.i + 1, 1)]
                    sp.dma_start(x_ln[:, :, :], nxt.rearrange("b (p h) d -> p (b h) d", h=T)).then_inc(x_in, 16)
                if f.off == 3:
                    if f.final:
                        sp.wait_ge(y_ready, 2 * LAST_ROUND)
                        src = x[LAST_ROUND:LAST_ROUND + 1]
                    else:
                        src = x[bass.ds(f.i, 1)]
                    sp.dma_start(x1[:, :, :], src.rearrange("b (p h) d -> p (b h) d", h=T)).then_inc(x1_in, 16)
                if not (f.final and f.off >= 2):
                    slot = (f.off + 2) % GROUPS
                    if not f.first:
                        if f.off >= 2:
                            sp.wait_ge(s2_full, f.count(CHUNKS, -CHUNKS))
                        if f.off == 2:
                            for side in range(2):
                                sp.wait_ge(lo_ready, f.per_round(4, 6 + 2 * side))
                                for n in range(PARTS):
                                    load_part(slot, side, n)
                    else:
                        sp.wait_ge(zeroed, GROUPS)
                    if f.off != 2:
                        load_qk(slot)
                if MAX_ROW[0] in f.uses:
                    sp.wait_ge(parts_ready, f.count(1, 2))
                    load_rows((f.off + 1) % GROUPS)
                if f.mix:
                    sp.wait_ge(y_ready, f.per_round(2, 2))
                    dst = out[bass.ds(f.i, 1)].rearrange("b (p h) d -> p (b h) d", h=T)
                    sp.dma_start(dst, y[:, :, :]).then_inc(out_done, 16)

            rounds(sp, phase)
            dst = out[LAST_ROUND].rearrange("(p h) d -> p h d", h=T)
            for u in range(2):
                sp.wait_ge(y_ready, 2 * LAST_ROUND + u + 1)
                sp.dma_start(dst[:, 4 * u:4 * u + 4, :], y[:, 4 * u:4 * u + 4, :]).then_inc(out_done, 16)
            sp.wait_ge(out_done, 16 * (B + 2))

        @block.gpsimd
        def _(pool):
            g = nc.gpsimd
            g.memset(ident[:, :], 0.0).then_inc(pool_setup, 1)
            g.memset(ident_bf[:, :], 0.0).then_inc(pool_setup, 1)
            g.memset(causal[:, :], 0.0).then_inc(pool_setup, 1)
            g.memset(minus_half[:, :], -0.5).then_inc(pool_setup, 1)
            g.memset(ones[:, :], 1.0).then_inc(consts_ready, 1)
            wait_apart(pool, pool_setup, 4)
            for m in (ident, ident_bf):
                g.affine_select(out=m[:, :], in_=m[:, :], compare_op=ALU.not_equal, fill=1.0, base=0,
                                pattern=[[-1, 128]], channel_multiplier=1).then_inc(consts_ready, 1)
            g.affine_select(out=causal[:, :], in_=causal[:, :], compare_op=ALU.is_ge, fill=LOW, base=0,
                            pattern=[[-1, 128]], channel_multiplier=1).then_inc(consts_ready, 1)

            def deviation(ln):
                wait_apart(pool, stats_ready, ln + 1)
                g.tensor_tensor(rstd[:, :], var_eps[:, :], minus_half[:, :], ALU.pow).then_inc(rstd_ready, 1)

            def third_part(side, half, n):
                dst = (q_parts, k_parts)[side]
                cols = slice(HALF * half, HALF * half + HALF)
                wait_apart(pool, mid_ready, n + 1)
                g.tensor_tensor(dst[:, 2, cols], rest[:, half, :], dst[:, 1, cols], ALU.subtract).then_inc(lo_ready, 1)

            def place_values(slot):
                src = v_all[:, :, 32 * slot:32 * slot + 32].rearrange("p t (n h) -> p t n h", h=H)
                g.tensor_copy(va[:, slot, :, :, 0:H], src).then_inc(v_ready, 1)

            deviation(0)
            g.memset(va[:, :, :, :, H + 1:VW], 0.0).then_inc(values_cleared, 1)
            g.memset(va[:, :, :, :, H:H + 1], 1.0).then_inc(values_cleared, 1)
            for n in range(4):
                third_part(n // 2, n % 2, n)
            wait_apart(pool, setup_copied, 4)
            place_values(0)
            place_values(1)

            def place_next(f):
                if not (f.final and f.off >= 2):
                    if f.off >= 2:
                        wait_apart(pool, sets_done, f.count(SETS, -SETS))
                    if f.off == 2:
                        wait_apart(pool, bank_read, f.use("v1") + 1)
                    place_values((f.off + 2) % GROUPS)

            def join_first(use, batches):
                wait_apart(pool, x1_in, batches)
                wait_apart(pool, bank_read, use + 1)
                g.tensor_tensor(x1[:, :, 0:JOINED], att[:, :, 0:JOINED], x1[:, :, 0:JOINED],
                                ALU.add).then_inc(joined, 1)

            def scale_k():
                g.tensor_scalar(xk[:, :], xT[:, 1:1 + S], mu[:, 1:2], 1.0, ALU.mult, ALU.mult).then_inc(scaled_k, 1)

            def square_k(half, use):
                cols = slice(HALF * half, HALF * half + HALF)
                wait_apart(pool, bank_read, use + 1)
                g.tensor_tensor(k_act[:, cols], k_relu[:, cols], k_relu[:, cols], ALU.mult).then_inc(act_ready, 1)

            def phase(f):
                if f.off != 2:
                    place_next(f)
                for step in range(CHUNKS):
                    if f.off == 2 and step == 16:
                        place_next(f)
                    if f.off == 3 and step == 14:
                        join_first(f.use(OT_LAST[0]), f.per_round(16, 16))
                    if step in DIAGONAL:
                        wait_apart(pool, exp_done, f.count(CHUNKS, step + 1))
                        blocks = probs[:, step % PSLOTS, :].rearrange("p (a c) -> p a c", c=128)
                        blocks = blocks[:, 0:4:DIAGONAL[step], :] if DIAGONAL[step] else blocks[:, 0:1, :]
                        g.affine_select(out=blocks, in_=blocks, compare_op=ALU.is_ge, fill=0.0, base=0,
                                        pattern=[[0, blocks.shape[1]], [1, 128]],
                                        channel_multiplier=-1).then_inc(masked, 1)
                    name = f.steps.get(step)
                    if f.project:
                        if f.project == 1 and step == 14:
                            deviation(f.per_round(2, 1))
                        if name and name.startswith("qk"):
                            n = int(name[2])
                            third_part(n // 2, n % 2, f.per_round(4, 4 + n))
                    if f.mix:
                        if step == 9:
                            deviation(f.per_round(2, 2))
                        if name == "xT1":
                            wait_apart(pool, bank_read, f.use("xT1") + 1)
                            scale_k()
                        if name in ("k0", "k1"):
                            square_k(int(name[1]), f.use(name))

            rounds(pool, phase)
            deviation(2 * LAST_ROUND + 1)
            wait_apart(pool, tail_done, 2)
            scale_k()

        @block.scalar
        def _(act):
            def copy_out(dst, src, use):
                act.wait_ge(bank_full, use + 1)
                nc.scalar.activation(dst, src, ACT.Copy).then_inc(bank_read, 1)

            def transposed_x(u, use):
                dst = xT[:, 1:1 + S].rearrange("d (p h) -> d h p", h=T)[:, 4 * u:4 * u + 4, :]
                copy_out(dst, shared[:, :].rearrange("d (h p) -> d h p", h=4), use)

            def two_parts(n, use):
                dst = (q_parts, k_parts)[n // 2]
                cols = slice(HALF * (n % 2), HALF * (n % 2) + HALF)
                act.wait_ge(bank_full, use + 1)
                nc.scalar.activation(dst[:, 0, cols], shared[:, :], ACT.Copy).then_inc(hi_ready, 1)
                act.wait_ge(bank_read, use + 1)
                nc.scalar.activation(dst[:, 1, cols], rest[:, n % 2, :], ACT.Copy).then_inc(mid_ready, 1)

            def tanh_gate(half, use):
                cols = slice(HALF * half, HALF * half + HALF)
                act.wait_ge(bank_full, use + 1)
                nc.scalar.activation(gate[:, cols], shared[:, :], ACT.Tanh, scale=0.5).then_inc(bank_read, 1)

            def relu_k(half, use):
                cols = slice(HALF * half, HALF * half + HALF)
                act.wait_ge(bank_full, use + 1)
                nc.scalar.activation(k_relu[:, cols], shared[:, :], ACT.Relu).then_inc(bank_read, 1)

            def zero_slot(slot):
                for dst, rows, value in ((qa, slice(64, 96), 0), (ka, slice(64, 96), 0), (ka, slice(96, ALL_ROWS), 1)):
                    flat = dst[rows, slot, :, :].rearrange("p h s -> p (h s)").bitcast(F32)
                    last = nc.scalar.activation(flat, fill[rows, value:value + 1].broadcast_to(list(flat.shape)), ACT.Copy)
                last.then_inc(zeroed, 1)

            def normalise(src, h, ready=None):
                if ready is not None:
                    act.wait_ge(shift_ready, ready)
                for t in (h, h + 1):
                    last = nc.scalar.activation(xn[:, t, :], src[:, t, :], ACT.Identity, scale=rstd[:, t:t + 1],
                                                bias=shift[:, t:t + 1])
                if h % 4 == 2:
                    last.then_inc(xn_ready, 1)

            act.wait_ge(fill_ready, 2)
            zero_slot(0)
            for h in (4, 6):
                normalise(x_ln, h, 1)
            for u in range(2):
                act.wait_ge(setup_full, u + 1)
                dst = xT[:, 1:1 + S].rearrange("d (p h) -> d h p", h=T)[:, 4 * u:4 * u + 4, :]
                nc.scalar.activation(dst, (bank2[2], acc)[u][:, :].rearrange("d (h p) -> d h p", h=4),
                                     ACT.Copy).then_inc(setup_copied, 1)
            for n in range(5):
                if n < 4:
                    act.wait_ge(setup_full, 2 + n + 1)
                    dst = (q_parts, k_parts)[n // 2]
                    nc.scalar.activation(dst[:, 0, HALF * (n % 2):HALF * (n % 2) + HALF], qk_banks[n][:, :],
                                         ACT.Copy).then_inc(hi_ready, 1)
                if n > 0:
                    m = n - 1
                    act.wait_ge(rest_done, m + 1)
                    dst = (q_parts, k_parts)[m // 2]
                    nc.scalar.activation(dst[:, 1, HALF * (m % 2):HALF * (m % 2) + HALF], rest[:, m % 2, :],
                                         ACT.Copy).then_inc(mid_ready, 1)
            for u in range(2):
                act.wait_ge(setup_full, 6 + u + 1)
                nc.scalar.activation(v_all[:, 4 * u:4 * u + 4, :].rearrange("p a b -> p (a b)"), bank2[u][:, :],
                                     ACT.Copy).then_inc(setup_copied, 1)
            zero_slot(1)
            act.wait_ge(setup_full, 9)
            nc.scalar.activation(w_sum[:, :], bank2[2][:, 0:D], ACT.Copy).then_inc(setup_copied, 1)
            act.wait_ge(setup_full, 10)
            nc.scalar.activation(w_mixT[:, :, :].rearrange("p a b -> p (a b)"), acc[:, 0:3 * D],
                                 ACT.Copy).then_inc(setup_copied, 1)
            zero_slot(2)
            zero_slot(3)

            def read_acc(f, sets):
                act.wait_ge(sets_done, sets)
                nc.scalar.activation(oT[:, :], acc[:, :], ACT.Copy).then_inc(acc_read, 1)

            def phase(f):
                for step in range(CHUNKS):
                    act.wait_ge(s2_full, f.count(CHUNKS, step + 1))
                    if step >= PSLOTS:
                        act.wait_ge(sets_done, f.count(SETS, set_of(step - PSLOTS) + 1))
                    elif not f.first:
                        act.wait_ge(sets_done, f.count(SETS, set_of(step - PSLOTS + CHUNKS) + 1 - SETS))
                    nc.scalar.activation(probs[:, step % PSLOTS, :], bank2[step % RING][:, :], ACT.Exp,
                                         scale=SCALE).then_inc(exp_done, 1)
                    if step == 2 and not f.first:
                        read_acc(f, f.count(SETS, 0))
                    if step == SET_ENDS[HALF_SETS - 1] + LAG:
                        if not f.first:
                            act.wait_ge(bank_full, f.use(OT_LAST[0]) + 1)
                        read_acc(f, f.count(SETS, HALF_SETS))
                    if f.project == 1 and 18 <= step < 22:
                        normalise(x_ln, 2 * (step - 18), f.per_round(2, 2))
                    if f.mix and 13 <= step < 17:
                        normalise(x1, 2 * (step - 13), f.per_round(2, 3))
                    if f.mix and step == 19:
                        act.wait_ge(bank_read, f.use("xT1") + 1)
                        nc.scalar.activation(scaled[:, :], xT[:, 1:1 + S], ACT.Copy, scale=mu[:, 0:1]).then_inc(scaled_r, 1)
                    if f.mix and step == 25:
                        act.wait_ge(bank_read, f.use("r1") + 1)
                        nc.scalar.activation(gate[:, :], gate[:, :], ACT.Copy, scale=0.5, bias=0.5).then_inc(gate_ready, 1)
                    name = f.steps.get(step)
                    if name in ("xT0", "xT1"):
                        transposed_x(int(name[2]), f.use(name))
                    elif f.project and name and name.startswith("qk"):
                        n = int(name[2])
                        if n == 0:
                            act.wait_ge(qk_in[(f.off + 2) % GROUPS], f.fills(2))
                        two_parts(n, f.use(name))
                    elif f.project and name in ("v0", "v1"):
                        u = int(name[1])
                        if u == 0:
                            act.wait_ge(v_ready, f.count(1, 2))
                        copy_out(v_all[:, 4 * u:4 * u + 4, :].rearrange("p a b -> p (a b)"), shared[:, :], f.use(name))
                    elif name in ("r0", "r1"):
                        tanh_gate(int(name[1]), f.use(name))
                    elif name in ("k0", "k1"):
                        relu_k(int(name[1]), f.use(name))

            rounds(act, phase)
            read_acc(None, SETS * B * GROUPS)
            for h in (4, 6):
                normalise(x1, h, 2 * B)
            for u in range(2):
                act.wait_ge(tail_full, u + 1)
                dst = xT[:, 1:1 + S].rearrange("d (p h) -> d h p", h=T)[:, 4 * u:4 * u + 4, :]
                nc.scalar.activation(dst, bank2[u][:, :].rearrange("d (h p) -> d h p", h=4),
                                     ACT.Copy).then_inc(tail_done, 1)
            act.wait_ge(tail_done, 2)
            for cols in halves:
                nc.scalar.activation(scaled[:, cols], xT[:, 1 + cols.start:1 + cols.stop], ACT.Copy,
                                     scale=mu[:, 0:1]).then_inc(tail_done, 1)
            for n, cols in enumerate(halves):
                act.wait_ge(tail_full, 2 + n + 1)
                nc.scalar.activation(gate[:, cols], (bank2[2], bank1[0])[n][:, :], ACT.Tanh,
                                     scale=0.5).then_inc(tail_done, 1)
            for n, cols in enumerate(halves):
                act.wait_ge(tail_full, 4 + n + 1)
                nc.scalar.activation(k_relu[:, cols], bank1[1 + n][:, :], ACT.Relu).then_inc(tail_done, 1)
            act.wait_ge(tail_done, 6)
            nc.scalar.activation(gate[:, :], gate[:, :], ACT.Copy, scale=0.5, bias=0.5).then_inc(tail_done, 1)

        @block.vector
        def _(dve):
            v = nc.vector

            def reduce_chunk(r, bank, done, first_ever):
                piece = PASS1[r][0]
                h, j = piece[0], piece[1]
                src = bank[:, :]
                if r < 16:
                    dst = far_max[:, h, j - 4:j - 3]
                elif r < 24:
                    dst = part_max[:, h, j, 0:1]
                elif r < 32:
                    dst = part_max[:, h, :, :].rearrange("p t c -> p (t c)")[:, 3 * j + 2:3 * j + 6]
                    src = src.rearrange("p (a c) -> p a c", c=128)
                else:
                    dst = part_max[:, h:h + 2, j + 1, 0]
                    src = src.rearrange("p (a c) -> p a c", c=256)
                dve.wait_ge(s1_full, done + 1)
                v.reduce_max(dst, src, AX.X).then_inc(s1_read, 1)

            def finish_max(groups, chunks):
                dve.wait_ge(s1_read, chunks)
                v.reduce_max(q_max[:, :].rearrange("p (g b a) -> p g a b", b=2, a=2),
                             part_max[:, :, :, :].rearrange("p h (c a b) k -> p (h c) a b k", a=2, b=2),
                             AX.X).then_inc(far_done, 1)
                dve.wait_ge(far_done, groups + 1)
                far = q_max[:, :].rearrange("p (h t) -> p h t", t=T)[:, :, 4:8]
                v.tensor_tensor(far, far, far_max[:, :, :], ALU.max).then_inc(max_ready, 1)
                dve.wait_ge(max_ready, groups + 1)

            def split_max(use, rows, steps):
                got = shared[0:GH * T, 0:128]
                dve.wait_ge(bank_full, use + 1)
                if rows is not None:
                    dve.wait_ge(rows_in, rows)
                v.tensor_scalar(neg_parts[:, 0, :], got, -1.0, None, ALU.mult).then_inc(split_step, 1)
                dve.wait_ge(split_step, steps + 1)
                v.scalar_tensor_tensor(neg_rest[:, :], got, -1.0, neg_parts[:, 0, :], ALU.mult,
                                       ALU.subtract).then_inc(bank_read, 1)
                dve.wait_ge(bank_read, use + 1)
                v.tensor_copy(neg_parts[:, 1, :], neg_rest[:, :]).then_inc(split_step, 1)
                dve.wait_ge(split_step, steps + 2)
                v.tensor_tensor(neg_parts[:, 2, :], neg_rest[:, :], neg_parts[:, 1, :], ALU.subtract).then_inc(parts_ready, 1)

            def bn(src, tiles):
                for h in tiles:
                    v.bn_stats(stats[:, h, :], src[:, h, :]).then_inc(bn_done, 1)

            def bn_end(ln):
                wait_apart(dve, bn_done, ln * (2 * T) + T)
                for h in range(T):
                    v.bn_aggr(mean_var[:, h, :], stats[:, h, :]).then_inc(bn_done, 1)
                wait_apart(dve, bn_done, ln * (2 * T) + 2 * T)
                v.tensor_scalar(var_eps[:, :], mean_var[:, :, 1], EPS, None, ALU.add).then_inc(stats_ready, 1)

            def shift_of(ln):
                dve.wait_ge(rstd_ready, ln + 1)
                v.scalar_tensor_tensor(shift[:, :], mean_var[:, :, 0], -1.0, rstd[:, :], ALU.mult,
                                       ALU.mult).then_inc(shift_ready, 1)

            def normalise_first(src, ready):
                dve.wait_ge(shift_ready, ready)
                for h in range(4):
                    last = v.tensor_scalar(xn[:, h, :], src[:, h, :], rstd[:, h:h + 1], shift[:, h:h + 1],
                                           ALU.mult, ALU.add)
                last.then_inc(xn_ready, 1)

            def rest_of(n, use):
                cols = slice(HALF * (n % 2), HALF * (n % 2) + HALF)
                dst = (q_parts, k_parts)[n // 2]
                v.tensor_tensor(rest[:, n % 2, :], shared[:, :], dst[:, 0, cols], ALU.subtract).then_inc(bank_read, 1)

            def normalise_out(slot, half, use, units):
                got = shared[:, :].rearrange("p (j n c) -> p j n c", j=4, n=GH)
                dve.wait_ge(bank_full, use + 1)
                v.reciprocal(inv[:, :, :], got[:, :, :, H]).then_inc(inv_step, 1)
                dve.wait_ge(inv_step, units * 2 + 1)
                w = w_sum[:, :].rearrange("p (n j) -> p j n", j=T)[:, 4 * half:4 * half + 4, GH * slot:GH * slot + GH]
                v.tensor_tensor(inv_w[:, :, :], inv[:, :, :], w, ALU.mult).then_inc(inv_step, 1)
                dve.wait_ge(inv_step, units * 2 + 2)
                dst = att[:, :, :].rearrange("p h (n j) -> p j n h", j=T)[:, 4 * half:4 * half + 4, GH * slot:GH * slot + GH, :]
                v.tensor_tensor(dst, got[:, :, :, 0:H], inv_w[:, :, :].unsqueeze(3).broadcast_to([128, 4, GH, H]),
                                ALU.mult).then_inc(bank_read, 1)

            def join_last(batches, use):
                wait_apart(dve, joined, batches + 1)
                dve.wait_ge(bank_read, use + 1)
                v.tensor_tensor(x1[:, :, JOINED:D], att[:, :, JOINED:D], x1[:, :, JOINED:D], ALU.add).then_inc(att_ready, 1)
                wait_apart(dve, att_ready, batches + 1)

            def mix_x(side, n):
                product = (scaled, xk)[side]
                dve.wait_ge((scaled_r, scaled_k)[side], n + 1)
                for cols in halves:
                    v.scalar_tensor_tensor((xr, xk)[side][:, cols], xT[:, cols], one_less_mu[:, side:side + 1],
                                           product[:, cols], ALU.mult, ALU.add).then_inc(mixed, 1)

            def gate_v(half, use):
                cols = slice(HALF * half, HALF * half + HALF)
                dve.wait_ge(bank_full, use + 1)
                v.tensor_tensor(yT[:, cols], shared[:, :], gate[:, cols], ALU.mult).then_inc(bank_read, 1)

            def add_y(u, use, stored):
                dve.wait_ge(bank_full, use + 1)
                if u == 0:
                    dve.wait_ge(out_done, stored)
                v.tensor_tensor(y[:, 4 * u:4 * u + 4, :], shared[:, :].rearrange("p (h d) -> p h d", h=4),
                                x1[:, 4 * u:4 * u + 4, :], ALU.add).then_inc(bank_read, 1)

            v.memset(fill[:, 0:1], 0.0).then_inc(fill_ready, 1)
            v.memset(fill[:, 1:2].bitcast(BF16), 1.0).then_inc(fill_ready, 1)
            v.memset(part_max[:, :, :, :], 3 * LOW)
            v.memset(xT[:, 0:1], 0.0).then_inc(column_ready, 1)
            dve.wait_ge(x_in, 16)
            bn(x_ln, range(T))
            bn_end(0)
            dve.wait_ge(w_in, 7 * 16)
            qkv = w_all[:, :, :].rearrange("p (g n) e -> p g e n", n=GH)
            v.tensor_copy(wq[:, :].rearrange("p (g e n) -> p g e n", e=H, n=GH), qkv[:, :, 0:H, :]).then_inc(w_ready, 1)
            v.tensor_copy(wk[:, :].rearrange("p (g e n) -> p g e n", e=H, n=GH), qkv[:, :, H:2 * H, :]).then_inc(w_ready, 1)
            v.tensor_copy(wv[:, :].rearrange("p (n h) -> p n h", h=H), w_all[:, :, 2 * H:3 * H]).then_inc(w_ready, 1)
            v.tensor_scalar(one_less_mu[:, :], mu[:, :], -1.0, 1.0, ALU.mult, ALU.add).then_inc(w_ready, 1)
            shift_of(0)
            normalise_first(x_ln, 1)
            for n in range(4):
                dve.wait_ge(hi_ready, n + 1)
                if n >= 2:
                    dve.wait_ge(lo_ready, n - 1)
                v.tensor_tensor(rest[:, n % 2, :], qk_banks[n][:, :], (q_parts, k_parts)[n // 2][:, 0, halves[n % 2]],
                                ALU.subtract).then_inc(rest_done, 1)
            for n in range(CHUNKS + AHEAD):
                reduce_chunk(n % CHUNKS, bank1[n % RING], n, True)
                if n == CHUNKS - 1:
                    finish_max(0, CHUNKS)
                if n == CHUNKS + 2:
                    split_max(0, None, 0)

            def phase(f):
                for step in range(CHUNKS):
                    ahead = f.first_pass(step)
                    if ahead:
                        groups, slot, r = ahead
                        reduce_chunk(r, bank1[r % RING], f.count(CHUNKS, groups * CHUNKS + r), False)
                        if r == CHUNKS - 1:
                            finish_max(f.count(1, groups), f.count(CHUNKS, (groups + 1) * CHUNKS))
                    name = f.steps.get(step)
                    if name == OT_LAST[0]:
                        normalise_out((f.off - 1) % GROUPS, 1, f.use(name), f.count(2, -1))
                    elif name == OT_FIRST[0]:
                        normalise_out(f.slot, 0, f.use(name), f.count(2, 0))
                    elif name == MAX_ROW[0]:
                        split_max(f.use(name), f.count(48, 48), f.count(2, 2))
                    elif f.project and name and name.startswith("qk"):
                        n = int(name[2])
                        dve.wait_ge(hi_ready, f.per_round(4, 4 + n + 1))
                        dve.wait_ge(lo_ready, f.per_round(4, 4 + n - 1))
                        rest_of(n, f.use(name))
                    elif f.mix and name in ("v0", "v1"):
                        dve.wait_ge(gate_ready, f.per_round(1, 1))
                        gate_v(int(name[1]), f.use(name))
                    elif f.mix and name in ("y0", "y1"):
                        add_y(int(name[1]), f.use(name), f.per_round(16, 16))
                        v_done(f.use(name) + 1)
                    if f.project == 1:
                        if step == 6:
                            dve.wait_ge(x_in, f.per_round(16, 32))
                        if 6 <= step < 6 + T:
                            bn(x_ln, (step - 6,))
                        if step == 6 + T:
                            bn_end(f.per_round(2, 1))
                        if step == 17:
                            shift_of(f.per_round(2, 1))
                    if f.mix:
                        if step == 6:
                            join_last(f.per_round(1, 0), f.use(OT_LAST[0]))
                        if 6 <= step < 10:
                            bn(x1, (2 * (step - 6), 2 * (step - 6) + 1))
                        if step == 9:
                            bn_end(f.per_round(2, 2))
                        if step == 12:
                            shift_of(f.per_round(2, 2))
                        if step in (20, 22):
                            mix_x((step - 20) // 2, f.per_round(1, 0))

            def v_done(use):
                dve.wait_ge(bank_read, use)
                dve.sem_inc(y_ready, 1)

            rounds(dve, phase)
            normalise_out(GROUPS - 1, 1, tail_use, 2 * B * GROUPS - 1)
            join_last(LAST_ROUND, tail_use)
            bn(x1, range(T))
            bn_end(2 * LAST_ROUND + 1)
            shift_of(2 * LAST_ROUND + 1)
            normalise_first(x1, 2 * B)
            for half, cols in enumerate(halves):
                dve.wait_ge(tail_done, 2 + half + 1)
                v.scalar_tensor_tensor(xr[:, cols], xT[:, cols], one_less_mu[:, 0:1], scaled[:, cols],
                                       ALU.mult, ALU.add).then_inc(mixed, 1)
            dve.wait_ge(scaled_k, B)
            for cols in halves:
                v.scalar_tensor_tensor(xk[:, cols], xT[:, cols], one_less_mu[:, 1:2], xk[:, cols],
                                       ALU.mult, ALU.add).then_inc(mixed, 1)
            for half, cols in enumerate(halves):
                dve.wait_ge(tail_done, 6 + half + 1)
                v.tensor_tensor(k_act[:, cols], k_relu[:, cols], k_relu[:, cols], ALU.mult).then_inc(act_ready, 1)
            dve.wait_ge(tail_done, 9)
            for half, cols in enumerate(halves):
                dve.wait_ge(tail_full, 6 + half + 1)
                v.tensor_tensor(yT[:, cols], (acc, bank2[0])[half][:, :], gate[:, cols], ALU.mult).then_inc(yT_ready, 1)
            dve.wait_ge(out_done, 16 * B)
            for u in range(2):
                dve.wait_ge(tail_full, 8 + u + 1)
                v.tensor_tensor(y[:, 4 * u:4 * u + 4, :], bank2[1 + u][:, :].rearrange("p (h d) -> p h d", h=4),
                                x1[:, 4 * u:4 * u + 4, :], ALU.add).then_inc(y_ready, 1)

        @block.tensor
        def _(pe):
            mm = nc.tensor.matmul

            def first_pass(slot, r, bank, done):
                if not (isinstance(done, int) and done < RING):
                    pe.wait_ge(s1_read, done + (1 - RING))
                for h, j, k0, n, at, diag in PASS1[r]:
                    last = mm(bank[:, at:at + n], qa[0:QK_ROWS, slot, h, 128 * j:128 * j + 128],
                              ka[0:QK_ROWS, slot, h, k0:k0 + n], start=True, stop=diag is None)
                    if diag is not None:
                        last = mm(bank[:, diag:diag + 128], ident_bf[:, :], causal[:, :], start=False, stop=True)
                last.then_inc(s1_full, 1)

            def second_pass(slot, c, bank):
                for h, i, q0, n, at in PASS2[c]:
                    last = mm(bank[:, at:at + n], ka[0:ALL_ROWS, slot, h, 128 * i:128 * i + 128],
                              qa[0:ALL_ROWS, slot, h, q0:q0 + n], start=True, stop=True)
                last.then_inc(s2_full, 1)

            def values(slot, k):
                pieces = pieces_of_set(k)
                for i, q0, n, heads in pieces:
                    at = q0 % HALF
                    for h, c, place in heads:
                        last = mm(acc[VW * h:VW * h + VW, at:at + n], va[:, slot, i, h, :],
                                  probs[:, c % PSLOTS, place:place + n], start=i == 0,
                                  stop=k in (HALF_SETS - 1, SETS - 1))
                last.then_inc(sets_done, 1)

            def transpose_out():
                for j in range(4):
                    last = nc.tensor.transpose(shared[:, 128 * j:128 * j + 128], oT[:, 128 * j:128 * j + 128], ident[:, :])
                last.then_inc(bank_full, 1)

            def transpose_max():
                nc.tensor.transpose(shared[0:GH * T, 0:128], q_max[:, :], ident[:, :]).then_inc(bank_full, 1)

            def transpose_x(u, bank):
                for h in range(4):
                    last = nc.tensor.transpose(bank[:, 128 * h:128 * h + 128], xn[:, 4 * u + h, :], ident[:, :])
                return last

            def project_qk(n, bank):
                return mm(bank[:, :], (wq, wk)[n // 2][:, :], xT[:, 1 + HALF * (n % 2):1 + HALF * (n % 2) + HALF],
                          start=True, stop=True)

            def project_v(u, bank):
                for t in range(4):
                    at = 1 + 128 * (4 * u + t)
                    last = mm(bank[:, 128 * t:128 * t + 128], xT[:, at:at + 128], wv[:, :], start=True, stop=True)
                return last

            def mix_product(n, src, half, bank):
                return mm(bank[:, :], w_mixT[:, n, :], src[:, halves[half]], start=True, stop=True)

            def transpose_y(u, bank):
                tiles = yT[:, :].rearrange("d (p h) -> d h p", h=T)
                for h in range(4):
                    last = nc.tensor.transpose(bank[:, 128 * h:128 * h + 128], tiles[:, 4 * u + h, :], ident[:, :])
                return last

            pe.wait_ge(consts_ready, 4)
            pe.wait_ge(xn_ready, 2)
            for u in range(2):
                transpose_x(u, (bank2[2], acc)[u]).then_inc(setup_full, 1)
            pe.wait_ge(w_ready, 4)
            pe.wait_ge(column_ready, 1)
            pe.wait_ge(setup_copied, 2)
            for n in range(4):
                project_qk(n, qk_banks[n]).then_inc(setup_full, 1)
            for u in range(2):
                project_v(u, bank2[u]).then_inc(setup_full, 1)
            pe.wait_ge(w_in, 7 * 16)
            mm(bank2[2][:, 0:D], ones[:, :], wo[:, :], start=True, stop=True).then_inc(setup_full, 1)
            for n in range(3):
                last = nc.tensor.transpose(acc[:, 128 * n:128 * n + 128], w_mix[:, n, :], ident[:, :])
            last.then_inc(setup_full, 1)
            for n in range(CHUNKS + AHEAD):
                if n % CHUNKS == 0:
                    pe.wait_ge(qk_in[n // CHUNKS], 16 * QK_DMAS)
                if n < RING:
                    pe.wait_ge(rest_done, n + 1)
                first_pass(n // CHUNKS, n % CHUNKS, bank1[n % RING], n)
                if n == CHUNKS + 2:
                    pe.wait_ge(max_ready, 1)
                    pe.wait_ge(rest_done, 4)
                    transpose_max()

            def phase(f):
                for step in range(CHUNKS):
                    if step == 0:
                        pe.wait_ge(rows_in, f.count(48, 48))
                    if f.first and step < RING:
                        pe.wait_ge(setup_copied, 3 + step)
                    else:
                        pe.wait_ge(exp_done, f.count(CHUNKS, step + 1 - RING))
                    second_pass(f.slot, step, bank2[step % RING])
                    ahead = f.first_pass(step)
                    if ahead:
                        groups, slot, r = ahead
                        if r == 0:
                            pe.wait_ge(qk_in[slot], f.fills(groups))
                        first_pass(slot, r, bank1[r % RING], f.count(CHUNKS, groups * CHUNKS + r))
                    if step - LAG in SET_ENDS:
                        k = SET_ENDS.index(step - LAG)
                        end = SET_ENDS[k]
                        pe.wait_ge(exp_done, f.count(CHUNKS, end + 1))
                        if end in DIAGONAL:
                            pe.wait_ge(masked, f.count(MASKS, masks_until(end)))
                        if k == 0:
                            pe.wait_ge(v_ready, f.count(1, 1))
                        if f.first and k == 0:
                            pe.wait_ge(setup_copied, 6)
                        elif k in (0, HALF_SETS):
                            pe.wait_ge(acc_read, f.count(2, int(k > 0)))
                        values(f.slot, k)
                    elif step - LAG + CHUNKS in SET_ENDS and not f.first:
                        k = SET_ENDS.index(step - LAG + CHUNKS)
                        end = SET_ENDS[k]
                        pe.wait_ge(exp_done, f.count(CHUNKS, end + 1 - CHUNKS))
                        pe.wait_ge(masked, f.count(MASKS, masks_until(end) - MASKS))
                        values((f.off - 1) % GROUPS, k)
                    name = f.steps.get(step)
                    if not name:
                        continue
                    pe.wait_ge(bank_read, f.use(name))
                    if name == OT_LAST[0]:
                        pe.wait_ge(acc_read, f.count(2, 0))
                        transpose_out()
                        continue
                    if name == OT_FIRST[0]:
                        pe.wait_ge(acc_read, f.count(2, 1))
                        transpose_out()
                        continue
                    if name == MAX_ROW[0]:
                        pe.wait_ge(max_ready, f.count(1, 2))
                        transpose_max()
                        continue
                    n = int(name[-1])
                    if name in ("xT0", "xT1"):
                        pe.wait_ge(xn_ready, f.per_round(4, 4 if f.project else 6))
                        last = transpose_x(n, shared)
                    elif name.startswith("qk"):
                        last = project_qk(n, shared)
                    elif f.project:
                        last = project_v(n, shared)
                    elif name in ("r0", "r1"):
                        pe.wait_ge(mixed, f.per_round(4, n + 1))
                        last = mix_product(0, xr, n, shared)
                    elif name in ("k0", "k1"):
                        pe.wait_ge(mixed, f.per_round(4, 2 + n + 1))
                        last = mix_product(1, xk, n, shared)
                    elif name in ("v0", "v1"):
                        pe.wait_ge(act_ready, f.per_round(2, n + 1))
                        last = mix_product(2, k_act, n, shared)
                    else:
                        last = transpose_y(n, shared)
                    last.then_inc(bank_full, 1)

            rounds(pe, phase)
            for k in (SETS - 2, SETS - 1):
                pe.wait_ge(exp_done, CHUNKS * (B * GROUPS - 1) + SET_ENDS[k] + 1)
                pe.wait_ge(masked, MASKS * (B * GROUPS - 1) + masks_until(SET_ENDS[k]))
                values(GROUPS - 1, k)
            pe.wait_ge(acc_read, 2 * B * GROUPS)
            pe.wait_ge(bank_read, tail_use)
            transpose_out()
            pe.wait_ge(xn_ready, 4 * B)
            for u in range(2):
                transpose_x(u, bank2[u]).then_inc(tail_full, 1)
            for half in range(2):
                pe.wait_ge(mixed, 4 * LAST_ROUND + half + 1)
                mix_product(0, xr, half, (bank2[2], bank1[0])[half]).then_inc(tail_full, 1)
            for half in range(2):
                pe.wait_ge(mixed, 4 * LAST_ROUND + 2 + half + 1)
                mix_product(1, xk, half, bank1[1 + half]).then_inc(tail_full, 1)
            for half in range(2):
                pe.wait_ge(act_ready, 2 * LAST_ROUND + half + 1)
                mix_product(2, k_act, half, (acc, bank2[0])[half]).then_inc(tail_full, 1)
            pe.wait_ge(yT_ready, 2)
            for u in range(2):
                transpose_y(u, bank2[1 + u]).then_inc(tail_full, 1)


def kernel(**inputs):
    import numpy as np
    import concourse.bacc as bacc
    from concourse.bass_utils import run_bass_kernel_spmd

    names = ["L0_attn_x", "L0_attn_W_qkv", "L0_attn_W_out", "L0_ffn_W_r", "L0_ffn_W_k", "L0_ffn_W_v",
             "L0_ffn_mu_r", "L0_ffn_mu_k"]
    nc = bacc.Bacc("TRN2", target_bir_lowering=False, num_devices=1)
    arrays, args = {}, []
    for name in names:
        a = np.ascontiguousarray(inputs[name])
        arrays[f"in_{name}"] = a
        args.append(nc.dram_tensor(f"in_{name}", a.shape, mybir.dt.from_np(a.dtype), kind="ExternalInput").ap())
    args.append(nc.dram_tensor("out_x", (B, S, D), F32, kind="ExternalOutput").ap())
    build(nc, *args)
    r = run_bass_kernel_spmd(nc, [arrays], core_ids=[0])
    return r.results[0]["out_x"]
```

```python
import concourse.bass as bass
import concourse.mybir as mybir
from contextlib import ExitStack

F32 = mybir.dt.float32
BF16 = mybir.dt.bfloat16
ALU = mybir.AluOpType
ACT = mybir.ActivationFunctionType
AX = mybir.AxisListType

B, S, D, N, H = 4, 1024, 128, 16, 8
T = S // 128
GH = 4
GROUPS = N // GH
HALF = S // 2
PARTS = 3
QK_ROWS = 96
ALL_ROWS = QK_ROWS + PARTS
VW = 32
CHUNKS = 36
AHEAD = 12
BY_VECTOR = 5
WARM = 22, 30, 6
LAG = 3
LATER = 1
RING = 3
PSLOTS = 12
SCALE = H ** -0.5
EPS = 1e-5
LOW = -1e30
QK_DMAS = 2 * PARTS * PARTS

def _pass2():
    chunks = []
    for half in range(2):
        base, t0 = half * HALF, half * 4
        for i in range(t0):
            chunks += [[(h, i, base, 512, 0)] for h in range(GH)]
        chunks += [[(h, t0, base, 512, 0)] for h in range(GH)]
        chunks += [[(h, t0 + 1, base + 128, 384, 0), (h, t0 + 3, base + 384, 128, 384)] for h in range(GH)]
        chunks += [[(h, t0 + 2, base + 256, 256, 256 * (h % 2)) for h in (p, p + 1)] for p in (0, 2)]
    return chunks


PASS2 = _pass2()
SET_ENDS = [3, 7, 9, 13, 17, 21, 25, 29, 33, 35]
SETS = len(SET_ENDS)
HALF_SETS = 3
DIAGONAL = {c: 0 for c in (0, 1, 2, 3, 26, 27, 28, 29)}
DIAGONAL |= {c: 3 for c in (4, 5, 6, 7, 30, 31, 32, 33)}
DIAGONAL |= {c: 2 for c in (8, 9, 34, 35)}
MASKS = len(DIAGONAL)
JOINED = D - D // GROUPS


def masks_until(c):
    return sum(x <= c for x in DIAGONAL)


def set_of(c):
    return next(k for k, e in enumerate(SET_ENDS) if e >= c)


def pieces_of_set(k):
    first = SET_ENDS[k - 1] + 1 if k else 0
    found = {}
    for c in range(first, SET_ENDS[k] + 1):
        for h, i, q0, n, at in PASS2[c]:
            found.setdefault((i, q0, n), []).append((h, c, at))
    return [(i, q0, n, hs) for (i, q0, n), hs in found.items()]


def _pass1():
    chunks = [[(h, j, 0, 512, 0)] for j in range(4, 8) for h in range(GH)]
    for j, k0 in ((1, 0), (5, 512)):
        chunks += [[(h, j, k0, 128, 0), (h, j + 2, k0, 384, 128)] for h in range(GH)]
    chunks += [[(h, 2, 0, 256, 0), (h, 6, 512, 256, 256)] for h in range(GH)]
    for j in range(T):
        chunks.insert(4 * j + 1, [(h, j, 128 * j, 128, 128 * h) for h in range(GH)])
    return chunks


PASS1 = _pass1()
ON_DIAGONAL = [4 * j + 1 for j in range(T)]
DIAG = T
PLAIN = CHUNKS - DIAG
DIAG_LAG = 4
PLACE = (0, 2, 1, 3, 4, 6, 5, 7)
assert all(PLACE[PLACE[t]] == t for t in range(T))


def chunks_before(r):
    groups, r = divmod(r, CHUNKS)
    diag = sum(x < r for x in ON_DIAGONAL)
    return groups * DIAG + diag, groups * PLAIN + r - diag


OT_LAST, OT_FIRST, MAX_ROW = "OUT, 2nd half of the group before", "OUT, 1st half", "MAX"
PLAIN_PHASE = {OT_LAST: 5, OT_FIRST: 15, MAX_ROW: 26, "join": 23}
PROJECT_1 = {OT_LAST: 5, OT_FIRST: 14, MAX_ROW: 26, "stats": 5, "deviation": 14, "shift": 15, "normalise": 16,
             "XT0": 24, "XT1": 28, "QK0": 30, "QK1": 33}
PROJECT_2 = {OT_LAST: 5, OT_FIRST: 18, MAX_ROW: 26, "QK2": 0, "QK3": 9, "V0": 11, "V1": 14, "place": 16}
MIX = {OT_LAST: 5, OT_FIRST: 14, MAX_ROW: 27, "join": 6, "stats": 6, "deviation": 14, "shift": 16,
       "normalise": 17, "XT0": 24, "XT1": 25, "scale r": 27, "scale k": 29, "mix r": 27, "mix k": 30, "R0": 30,
       "R1": 31, "gate": 34, "K0": 33, "K1": 35}
FINISH = {"W0": 1, "W1": 7, "Y0": 11, "Y1": 12}


def uses_of(events):
    uses = sorted((step, name) for name, step in events.items() if name.isupper() or "OUT" in name)
    return {name: n for n, (_, name) in enumerate(uses)}


FIRST_USES = 1 + 2
USES_BEFORE = {0: -2, 1: 0, 2: len(uses_of(PROJECT_1))}
USES_BEFORE[3] = USES_BEFORE[2] + len(uses_of(PROJECT_2))
USES_BEFORE[4] = USES_BEFORE[3] + 3
ROUND_USES = USES_BEFORE[4] + len(uses_of(MIX)) + len(uses_of(FINISH))


class Phase:

    def __init__(self, i, off, project=0, mix=False, finish=False, first=False, last=False, eng=None, products=None):
        self.i, self.off, self.project, self.mix = i, off, project, mix
        self.eng, self.products = eng, products
        self.first, self.last = first, last
        self.final = isinstance(i, int) and i == LAST_ROUND
        self.slot = off % GROUPS
        self.finish = finish
        events = MIX if mix else {0: PLAIN_PHASE, 1: PROJECT_1, 2: PROJECT_2}[project]
        if finish:
            events = {**events, **FINISH}
            assert len(set(events[name] for name in uses_of(events))) == len(uses_of(events))
        skipped = [OT_LAST] * first + [MAX_ROW] * last
        self.events = {name: step for name, step in events.items() if name not in skipped}
        self.uses = uses_of(self.events)
        self.steps = {self.events[name]: name for name in self.uses}
        self.before = {1: -4, 2: 3, 3: 6}[off] if self.final else USES_BEFORE[off] - 4 * finish

    def per_round(self, each, more):
        if isinstance(self.i, int):
            return self.i * each + more
        if each not in self.products:
            self.products[each] = self.eng.snap(self.i * each)
        return self.products[each] + more

    def count(self, per_group, more):
        return self.per_round(GROUPS * per_group, self.off * per_group + more)

    def fills(self, ahead):
        return self.per_round(16 * QK_DMAS, 16 * QK_DMAS * ((self.off + ahead) // GROUPS + 1))

    def use(self, name):
        return self.per_round(ROUND_USES, FIRST_USES + self.before + self.uses[name])

    def first_pass(self, step):
        n = step + AHEAD
        ahead, r = 1 + n // CHUNKS, n % CHUNKS
        if self.last or (self.final and self.off + ahead >= GROUPS):
            return None
        return ahead, (self.off + ahead) % GROUPS, r


    def diagonal(self, ahead):
        groups, _, r = ahead
        return self.count(DIAG, chunks_before(groups * CHUNKS + r)[0])

    def plain(self, ahead):
        groups, _, r = ahead
        return self.count(PLAIN, chunks_before(groups * CHUNKS + r)[1])


LAST_ROUND = B - 1


def build(nc, x, w_qkv, w_out, w_r, w_k, w_v, mu_r, mu_k, out):
    nc.disable_value_cache = True
    ctx = ExitStack()
    with ctx:
        def sb(name, shape, dt=F32):
            return ctx.enter_context(nc.sbuf_tensor(name, shape, dt))

        def ps(name):
            return ctx.enter_context(nc.psum_tensor(name, [128, 512], F32))

        def sem(name):
            return ctx.enter_context(nc.semaphore(name))

        qa = sb("qa", [128, GROUPS, GH, S], BF16)
        ka = sb("ka", [128, GROUPS, GH, S], BF16)
        va = sb("va", [128, GROUPS, T, GH, VW])
        probs = sb("probs", [128, PSLOTS, 512])
        q_parts = sb("q_parts", [128, PARTS, S], BF16)
        k_parts = sb("k_parts", [128, PARTS, S], BF16)
        v_all = sb("v_all", [128, T, D])
        x_ln = sb("x_ln", [128, T, D])
        x1 = sb("x1", [128, T, D])
        att = sb("att", [128, T, D])
        xn = sb("xn", [128, T, D])
        xT = sb("xT", [128, 1 + S])
        scaled = sb("scaled", [128, S])
        xr = sb("xr", [128, S])
        xk = sb("xk", [128, S])
        gate = sb("gate", [128, S])
        k_relu = sb("k_relu", [128, S])
        k_act = sb("k_act", [128, S])
        yT = sb("yT", [128, S])
        y = sb("y", [128, T, D])
        fill = sb("fill", [128, 2])
        rest = sb("rest", [128, 2, 512])
        oT = sb("oT", [128, 512])
        inv = sb("inv", [128, 4, GH])
        inv_w = sb("inv_w", [128, 4, GH])
        part_max = sb("part_max", [128, GH, T, 5])
        diag = sb("diag", [128, 2, GH, 128])
        q_max = sb("q_max", [128, GH * T])
        neg_rest = sb("neg_rest", [GH * T, 128])
        neg_parts = sb("neg_parts", [GH * T, PARTS, 128], BF16)
        stats = sb("stats", [128, T, 6])
        mean_var = sb("mean_var", [128, T, 2])
        var_eps = sb("var_eps", [128, T])
        rstd = sb("rstd", [128, T])
        shift = sb("shift", [128, T])
        minus_half = sb("minus_half", [128, T])
        w_all = sb("w_all", [128, N, 3 * H])
        wq = sb("wq", [128, D])
        wk = sb("wk", [128, D])
        wv = sb("wv", [128, D])
        wo = sb("wo", [128, D])
        w_sum = sb("w_sum", [128, D])
        w_mix = sb("w_mix", [128, 3, D])
        w_mixT = sb("w_mixT", [128, 3, D])
        mu = sb("mu", [128, 2])
        one_less_mu = sb("one_less_mu", [128, 2])
        ident = sb("ident", [128, 128])
        ones = sb("ones", [128, 128])

        bank2 = [ps(f"scores2_{n}") for n in range(RING)]
        bank1 = [ps(f"scores1_{n}") for n in range(RING)]
        acc = ps("acc")
        shared = ps("shared")

        x_half_in = [sem(f"x_half_in{n}") for n in range(2)]
        x_in = sem("x_in")
        w_in = sem("w_in")
        x1_in = sem("x1_in")
        qk_in = [sem(f"qk_in{n}") for n in range(GROUPS)]
        rows_in = sem("rows_in")
        out_done = sem("out_done")
        pool_setup = sem("pool_setup")
        consts_ready = sem("consts_ready")
        fill_ready = sem("fill_ready")
        zeroed = sem("zeroed")
        column_ready = sem("column_ready")
        w_ready = sem("w_ready")
        setup_full = sem("setup_full")
        setup_copied = sem("setup_copied")
        rest_done = sem("rest_done")
        tail_full = sem("tail_full")
        tail_done = sem("tail_done")
        rstd_ready = sem("rstd_ready")
        shift_ready = sem("shift_ready")
        bn_done = sem("bn_done")
        stats_ready = sem("stats_ready")
        xn_ready = sem("xn_ready")
        bank_full = sem("bank_full")
        bank_read = sem("bank_read")
        hi_ready = sem("hi_ready")
        mid_ready = sem("mid_ready")
        lo_ready = sem("lo_ready")
        v_ready = sem("v_ready")
        s1_full = sem("s1_full")
        s1_read = sem("s1_read")
        diag_copied = sem("diag_copied")
        diag_masked = sem("diag_masked")
        diag_done = sem("diag_done")
        max_ready = sem("max_ready")
        split_step = sem("split_step")
        parts_ready = sem("parts_ready")
        s2_full = sem("s2_full")
        exp_done = sem("exp_done")
        masked = sem("masked")
        sets_done = sem("sets_done")
        acc_read = sem("acc_read")
        inv_step = sem("inv_step")
        joined = sem("joined")
        att_ready = sem("att_ready")
        scaled_r = sem("scaled_r")
        scaled_k = sem("scaled_k")
        mixed = sem("mixed")
        gate_ready = sem("gate_ready")
        yT_ready = sem("yT_ready")
        act_ready = sem("act_ready")
        y_ready = sem("y_ready")

        values_cleared = sem("values_cleared")
        pool_passed = sem("pool_passed")
        dve_passed = sem("dve_passed")

        block = ctx.enter_context(nc.Block())

        def wait_apart(eng, sem, value):
            eng.wait_ge(sem, value)
            if not isinstance(value, int):
                eng.sem_inc(pool_passed if eng is nc.gpsimd else dve_passed, 1)

        def rounds(eng, phase):
            def four_phases(i, finish, multiples):
                phase(Phase(i, 1, project=1, finish=finish, eng=eng, products=multiples))
                phase(Phase(i, 2, project=2, eng=eng, products=multiples))
                phase(Phase(i, 3, eng=eng, products=multiples))
                phase(Phase(i, 4, mix=True, eng=eng, products=multiples))

            phase(Phase(0, 0, first=True))
            four_phases(0, False, None)
            with eng.Fori(1, B - 1) as i:
                four_phases(i, True, {})
            for off in (1, 2, 3):
                phase(Phase(LAST_ROUND, off, finish=off == 1, last=off == 3))

        tail_use = LAST_ROUND * ROUND_USES + FIRST_USES + 3 + 3 + 2
        halves = (slice(0, HALF), slice(HALF, S))

        def banks_for_second(f):
            return (bank2 + bank1 if f.last else bank2 + bank2) * (CHUNKS // (2 * RING))

        qk_banks = bank1 + [shared]

        @block.sync
        def _(sp):
            def load_part(slot, side, n):
                rows = slice(32 * slot, 32 * slot + 32)
                for m in range(PARTS):
                    at = H * (PARTS * m + n if side else PARTS * n + m)
                    sp.dma_start((qa, ka)[side][at:at + H, slot, :, :],
                                 (q_parts, k_parts)[side][rows, n, :]).then_inc(qk_in[slot], 16)

            def load_qk(slot):
                for side in range(2):
                    for n in range(PARTS):
                        load_part(slot, side, n)

            def load_rows(slot):
                for a in range(PARTS):
                    dst = qa[QK_ROWS + a:QK_ROWS + a + 1, slot, :, :].rearrange("a h (j s) -> a (h j) s", s=128)
                    sp.dma_start(dst, neg_parts[:, a, :]).then_inc(rows_in, 16)

            sp.sem_inc(out_done, 16)
            for u in range(2):
                sp.dma_start(x_ln[:, 4 * u:4 * u + 4, :],
                             x[0].rearrange("(p h) d -> p h d", h=T)[:, 4 * u:4 * u + 4, :]).then_inc(x_half_in[u], 16)
            sp.dma_start(w_all[:, :, :], w_qkv.rearrange("n d e -> d n e")).then_inc(w_in, 16)
            sp.dma_start(wo[:, :], w_out.rearrange("n h d -> (n h) d")).then_inc(w_in, 16)
            for n, w in enumerate((w_r, w_k, w_v)):
                sp.dma_start(w_mix[:, n, :], w[:, :]).then_inc(w_in, 16)
            for n, m in enumerate((mu_r, mu_k)):
                sp.dma_start(mu[:, n:n + 1], m.rearrange("(d o) -> d o", o=1)).then_inc(w_in, 16)
            sp.wait_ge(zeroed, 1)
            for side in range(2):
                for n, part_ready in enumerate((hi_ready, mid_ready, lo_ready)):
                    sp.wait_ge(part_ready, 2 * side + 2)
                    load_part(0, side, n)
            sp.wait_ge(zeroed, 2)
            load_qk(1)
            sp.wait_ge(parts_ready, 1)
            load_rows(0)

            def phase(f):
                if f.project == 1:
                    sp.wait_ge(xn_ready, f.per_round(4, 2))
                    nxt = x[1:2] if isinstance(f.i, int) else x[bass.ds(f.i + 1, 1)]
                    sp.dma_start(x_ln[:, :, :], nxt.rearrange("b (p h) d -> p (b h) d", h=T)).then_inc(x_in, 16)
                if f.off == 3:
                    if not (isinstance(f.i, int) and f.i == 0):
                        sp.wait_ge(y_ready, f.per_round(2, 0))
                    src = x[f.i:f.i + 1] if isinstance(f.i, int) else x[bass.ds(f.i, 1)]
                    sp.dma_start(x1[:, :, :], src.rearrange("b (p h) d -> p (b h) d", h=T)).then_inc(x1_in, 16)
                if not (f.final and f.off >= 2):
                    slot = (f.off + 2) % GROUPS
                    if not f.first:
                        if f.off >= 2:
                            sp.wait_ge(s2_full, f.count(CHUNKS, -CHUNKS))
                        if f.off == 2:
                            for side in range(2):
                                sp.wait_ge(lo_ready, f.per_round(4, 6 + 2 * side))
                                for n in range(PARTS):
                                    load_part(slot, side, n)
                    else:
                        sp.wait_ge(zeroed, GROUPS)
                    if f.off != 2:
                        load_qk(slot)
                if MAX_ROW in f.uses:
                    sp.wait_ge(parts_ready, f.count(1, 2))
                    load_rows((f.off + 1) % GROUPS)
                if f.finish:
                    sp.wait_ge(y_ready, f.per_round(2, 0))
                    dst = out[LAST_ROUND - 1:LAST_ROUND] if f.final else out[bass.ds(f.i - 1, 1)]
                    dst = dst.rearrange("b (p h) d -> p (b h) d", h=T)
                    sp.dma_start(dst, y[:, :, :]).then_inc(out_done, 16)

            rounds(sp, phase)
            dst = out[LAST_ROUND].rearrange("(p h) d -> p h d", h=T)
            for u in range(2):
                sp.wait_ge(y_ready, 2 * LAST_ROUND + u + 1)
                sp.dma_start(dst[:, 4 * u:4 * u + 4, :], y[:, 4 * u:4 * u + 4, :]).then_inc(out_done, 16)
            sp.wait_ge(out_done, 16 * (B + 2))

        @block.gpsimd
        def _(pool):
            g = nc.gpsimd
            g.memset(ident[:, :], 0.0).then_inc(pool_setup, 1)
            g.memset(minus_half[:, :], -0.5).then_inc(pool_setup, 1)
            g.memset(ones[:, :], 1.0).then_inc(consts_ready, 1)
            wait_apart(pool, pool_setup, 2)
            g.affine_select(out=ident[:, :], in_=ident[:, :], compare_op=ALU.not_equal, fill=1.0, base=0,
                            pattern=[[-1, 128]], channel_multiplier=1).then_inc(consts_ready, 1)

            def deviation(ln):
                wait_apart(pool, stats_ready, ln + 1)
                g.tensor_tensor(rstd[:, :], var_eps[:, :], minus_half[:, :], ALU.pow).then_inc(rstd_ready, 1)

            def third_part(side, half, n):
                dst = (q_parts, k_parts)[side]
                cols = slice(HALF * half, HALF * half + HALF)
                wait_apart(pool, mid_ready, n + 1)
                g.tensor_tensor(dst[:, 2, cols], rest[:, half, :], dst[:, 1, cols], ALU.subtract).then_inc(lo_ready, 1)

            def place_values(slot):
                src = v_all[:, :, 32 * slot:32 * slot + 32].rearrange("p t (n h) -> p t n h", h=H)
                g.tensor_copy(va[:, slot, :, :, 0:H], src).then_inc(v_ready, 1)

            deviation(0)
            g.memset(va[:, :, :, :, H + 1:VW], 0.0).then_inc(values_cleared, 1)
            g.memset(va[:, :, :, :, H:H + 1], 1.0).then_inc(values_cleared, 1)
            for n in range(4):
                third_part(n // 2, n % 2, n)
            wait_apart(pool, setup_copied, 4)
            place_values(0)
            place_values(1)

            def mask_diag(j, done):
                wait_apart(pool, diag_copied, done + 1)
                g.affine_select(out=diag[:, j % 2, :, :], in_=diag[:, j % 2, :, :], compare_op=ALU.is_ge, fill=LOW,
                                base=0, pattern=[[0, GH], [-1, 128]], channel_multiplier=1).then_inc(diag_masked, 1)

            for n in range(CHUNKS + AHEAD):
                if n % CHUNKS in ON_DIAGONAL:
                    mask_diag(ON_DIAGONAL.index(n % CHUNKS), chunks_before(n)[0])

            def place_next(f):
                if not (f.final and f.off >= 2):
                    if f.off >= 2:
                        wait_apart(pool, sets_done, f.count(SETS, -SETS))
                    if f.project == 2:
                        wait_apart(pool, bank_read, f.use("V1") + 1)
                    place_values((f.off + 2) % GROUPS)

            def join_first(use, batches):
                wait_apart(pool, x1_in, batches)
                wait_apart(pool, bank_read, use + 1)
                g.tensor_tensor(x1[:, :, 0:JOINED], att[:, :, 0:JOINED], x1[:, :, 0:JOINED],
                                ALU.add).then_inc(joined, 1)

            def scale_k():
                g.tensor_scalar(xk[:, :], xT[:, 1:1 + S], mu[:, 1:2], 1.0, ALU.mult, ALU.mult).then_inc(scaled_k, 1)

            def square_k(half, use):
                cols = slice(HALF * half, HALF * half + HALF)
                wait_apart(pool, bank_read, use + 1)
                g.tensor_tensor(k_act[:, cols], k_relu[:, cols], k_relu[:, cols], ALU.mult).then_inc(act_ready, 1)

            def phase(f):
                if "place" not in f.events:
                    place_next(f)
                for step in range(CHUNKS):
                    if step == f.events.get("place"):
                        place_next(f)
                    if f.off == 3 and step == f.events["join"]:
                        join_first(f.use(OT_LAST), f.per_round(16, 16))
                    if step in DIAGONAL:
                        wait_apart(pool, exp_done, f.count(CHUNKS, step + 1))
                        blocks = probs[:, step % PSLOTS, :].rearrange("p (a c) -> p a c", c=128)
                        blocks = blocks[:, 0:4:DIAGONAL[step], :] if DIAGONAL[step] else blocks[:, 0:1, :]
                        g.affine_select(out=blocks, in_=blocks, compare_op=ALU.is_ge, fill=0.0, base=0,
                                        pattern=[[0, blocks.shape[1]], [1, 128]],
                                        channel_multiplier=-1).then_inc(masked, 1)
                    ahead = f.first_pass(step)
                    if ahead and ahead[2] in ON_DIAGONAL:
                        mask_diag(ON_DIAGONAL.index(ahead[2]), f.diagonal(ahead))
                    name = f.steps.get(step)
                    if step == f.events.get("deviation"):
                        deviation(f.per_round(2, 1 if f.project else 2))
                    tile = step - f.events.get("normalise", CHUNKS)
                    if tile == 0:
                        wait_apart(pool, shift_ready, f.per_round(2, 2 if f.project else 3))
                    if 0 <= tile < T:
                        last = g.tensor_scalar(xn[:, tile, :], (x_ln if f.project else x1)[:, tile, :],
                                               rstd[:, tile:tile + 1], shift[:, tile:tile + 1], ALU.mult, ALU.add)
                        if tile % 4 == 3:
                            last.then_inc(xn_ready, 1)
                    if f.project:
                        if name and name.startswith("QK"):
                            n = int(name[2])
                            third_part(n // 2, n % 2, f.per_round(4, 4 + n))
                    if f.mix:
                        if step == f.events["scale k"]:
                            wait_apart(pool, bank_read, f.use("XT1") + 1)
                            scale_k()
                        if name in ("K0", "K1"):
                            square_k(int(name[1]), f.use(name))

            rounds(pool, phase)
            deviation(2 * LAST_ROUND + 1)
            wait_apart(pool, tail_done, 2)
            g.tensor_scalar(xr[:, :], xT[:, 1:1 + S], mu[:, 0:1], 1.0, ALU.mult, ALU.mult).then_inc(scaled_k, 1)

        @block.scalar
        def _(act):
            def copy_out(dst, src, use):
                act.wait_ge(bank_full, use + 1)
                nc.scalar.activation(dst, src, ACT.Copy).then_inc(bank_read, 1)

            def transposed_x(u, use):
                dst = xT[:, 1:1 + S].rearrange("d (p h) -> d h p", h=T)[:, 4 * u:4 * u + 4, :]
                copy_out(dst, shared[:, :].rearrange("d (h p) -> d h p", h=4), use)

            def two_parts(n, use):
                dst = (q_parts, k_parts)[n // 2]
                cols = slice(HALF * (n % 2), HALF * (n % 2) + HALF)
                act.wait_ge(bank_full, use + 1)
                nc.scalar.activation(dst[:, 0, cols], shared[:, :], ACT.Copy).then_inc(hi_ready, 1)
                act.wait_ge(bank_read, use + 1)
                nc.scalar.activation(dst[:, 1, cols], rest[:, n % 2, :], ACT.Copy).then_inc(mid_ready, 1)

            def tanh_gate(half, use):
                cols = slice(HALF * half, HALF * half + HALF)
                act.wait_ge(bank_full, use + 1)
                nc.scalar.activation(gate[:, cols], shared[:, :], ACT.Tanh, scale=0.5).then_inc(bank_read, 1)

            def relu_k(half, use):
                cols = slice(HALF * half, HALF * half + HALF)
                act.wait_ge(bank_full, use + 1)
                nc.scalar.activation(k_relu[:, cols], shared[:, :], ACT.Relu).then_inc(bank_read, 1)

            def zero_rows(slot, n):
                dst, rows, value = ((qa, slice(64, 96), 0), (ka, slice(64, 96), 0), (ka, slice(96, ALL_ROWS), 1))[n]
                flat = dst[rows, slot, :, :].rearrange("p h s -> p (h s)").bitcast(F32)
                last = nc.scalar.activation(flat, fill[rows, value:value + 1].broadcast_to(list(flat.shape)), ACT.Copy)
                if n == 2:
                    last.then_inc(zeroed, 1)

            def zero_slot(slot):
                for n in range(3):
                    zero_rows(slot, n)

            def copy_diag(j, bank, chunks, done):
                act.wait_ge(s1_full, chunks + 1)
                if not (isinstance(done, int) and done < 2):
                    act.wait_ge(diag_done, done - 1)
                nc.scalar.activation(diag[:, j % 2, :, :].rearrange("p a b -> p (a b)"), bank[:, :],
                                     ACT.Copy).then_inc(diag_copied, 1)

            def normalise_last(src, ready):
                act.wait_ge(shift_ready, ready)
                for h in range(BY_VECTOR, T):
                    last = nc.scalar.activation(xn[:, h, :], src[:, h, :], ACT.Identity, scale=rstd[:, h:h + 1],
                                                bias=shift[:, h:h + 1])
                last.then_inc(xn_ready, 1)

            act.wait_ge(fill_ready, 2)
            zero_slot(0)
            normalise_last(x_ln, 1)
            for u in range(2):
                act.wait_ge(setup_full, u + 1)
                dst = xT[:, 1:1 + S].rearrange("d (p h) -> d h p", h=T)[:, 4 * u:4 * u + 4, :]
                nc.scalar.activation(dst, (bank2[2], acc)[u][:, :].rearrange("d (h p) -> d h p", h=4),
                                     ACT.Copy).then_inc(setup_copied, 1)
            for n in range(5):
                if n < 4:
                    act.wait_ge(setup_full, 2 + n + 1)
                    dst = (q_parts, k_parts)[n // 2]
                    nc.scalar.activation(dst[:, 0, HALF * (n % 2):HALF * (n % 2) + HALF], qk_banks[n][:, :],
                                         ACT.Copy).then_inc(hi_ready, 1)
                if n > 0:
                    m = n - 1
                    act.wait_ge(rest_done, m + 1)
                    dst = (q_parts, k_parts)[m // 2]
                    nc.scalar.activation(dst[:, 1, HALF * (m % 2):HALF * (m % 2) + HALF], rest[:, m % 2, :],
                                         ACT.Copy).then_inc(mid_ready, 1)
            for u in range(2):
                act.wait_ge(setup_full, 6 + u + 1)
                nc.scalar.activation(v_all[:, 4 * u:4 * u + 4, :].rearrange("p a b -> p (a b)"), bank2[u][:, :],
                                     ACT.Copy).then_inc(setup_copied, 1)
            zero_slot(1)
            act.wait_ge(setup_full, 9)
            nc.scalar.activation(w_sum[:, :], bank2[2][:, 0:D], ACT.Copy).then_inc(setup_copied, 1)
            act.wait_ge(setup_full, 10)
            nc.scalar.activation(w_mixT[:, :, :].rearrange("p a b -> p (a b)"), acc[:, 0:3 * D],
                                 ACT.Copy).then_inc(setup_copied, 1)
            others = [(slot, n) for slot in (2, 3) for n in range(3)]
            for n in range(CHUNKS + AHEAD):
                if n % CHUNKS in ON_DIAGONAL:
                    if others:
                        zero_rows(*others.pop(0))
                    copy_diag(ON_DIAGONAL.index(n % CHUNKS), bank1[n % RING], n, chunks_before(n)[0])

            def read_acc(f, sets):
                act.wait_ge(sets_done, sets)
                nc.scalar.activation(oT[:, :], acc[:, :], ACT.Copy).then_inc(acc_read, 1)

            def phase(f):
                for step in range(CHUNKS):
                    act.wait_ge(s2_full, f.count(CHUNKS, step + 1))
                    if step >= PSLOTS:
                        act.wait_ge(sets_done, f.count(SETS, set_of(step - PSLOTS) + 1))
                    elif not f.first:
                        act.wait_ge(sets_done, f.count(SETS, set_of(step - PSLOTS + CHUNKS) + 1 - SETS))
                    nc.scalar.activation(probs[:, step % PSLOTS, :], banks_for_second(f)[step][:, :], ACT.Exp,
                                         scale=SCALE).then_inc(exp_done, 1)
                    if step == 2 and not f.first:
                        read_acc(f, f.count(SETS, 0))
                    if step == SET_ENDS[HALF_SETS - 1] + LAG + LATER * f.last:
                        if not f.first:
                            act.wait_ge(bank_full, f.use(OT_LAST) + 1)
                        read_acc(f, f.count(SETS, HALF_SETS))
                    ahead = f.first_pass(step)
                    if ahead and ahead[2] in ON_DIAGONAL:
                        groups, _, r = ahead
                        copy_diag(ON_DIAGONAL.index(r), bank1[r % RING], f.count(CHUNKS, groups * CHUNKS + r),
                                  f.diagonal(ahead))
                    if step == f.events.get("scale r"):
                        act.wait_ge(bank_read, f.use("XT1") + 1)
                        nc.scalar.activation(scaled[:, :], xT[:, 1:1 + S], ACT.Copy, scale=mu[:, 0:1]).then_inc(scaled_r, 1)
                    if step == f.events.get("gate"):
                        act.wait_ge(bank_read, f.use("R1") + 1)
                        nc.scalar.activation(gate[:, :], gate[:, :], ACT.Copy, scale=0.5, bias=0.5).then_inc(gate_ready, 1)
                    name = f.steps.get(step)
                    if name in ("XT0", "XT1"):
                        transposed_x(int(name[2]), f.use(name))
                    elif f.project and name and name.startswith("QK"):
                        n = int(name[2])
                        if n == 0:
                            act.wait_ge(qk_in[(f.off + 2) % GROUPS], f.fills(2))
                        two_parts(n, f.use(name))
                    elif f.project and name in ("V0", "V1"):
                        u = int(name[1])
                        if u == 0:
                            act.wait_ge(v_ready, f.count(1, 2))
                        copy_out(v_all[:, 4 * u:4 * u + 4, :].rearrange("p a b -> p (a b)"), shared[:, :], f.use(name))
                    elif name in ("R0", "R1"):
                        tanh_gate(int(name[1]), f.use(name))
                    elif name in ("K0", "K1"):
                        relu_k(int(name[1]), f.use(name))

            rounds(act, phase)
            read_acc(None, SETS * B * GROUPS)
            normalise_last(x1, 2 * B)
            for u in range(2):
                act.wait_ge(tail_full, u + 1)
                dst = xT[:, 1:1 + S].rearrange("d (p h) -> d h p", h=T)[:, 4 * u:4 * u + 4, :]
                nc.scalar.activation(dst, bank2[u][:, :].rearrange("d (h p) -> d h p", h=4),
                                     ACT.Copy).then_inc(tail_done, 1)
            act.wait_ge(tail_done, 2)
            for cols in halves:
                nc.scalar.activation(scaled[:, cols], xT[:, 1 + cols.start:1 + cols.stop], ACT.Copy,
                                     scale=mu[:, 1:2]).then_inc(tail_done, 1)
            for n, cols in enumerate(halves):
                act.wait_ge(tail_full, 2 + n + 1)
                nc.scalar.activation(k_relu[:, cols], bank1[1 + n][:, :], ACT.Relu).then_inc(tail_done, 1)
            for n, cols in enumerate(halves):
                act.wait_ge(tail_full, 4 + n + 1)
                nc.scalar.activation(gate[:, cols], (bank2[2], bank1[0])[n][:, :], ACT.Tanh,
                                     scale=0.5).then_inc(tail_done, 1)
                act.wait_ge(tail_done, 6 + 2 * n + 1)
                nc.scalar.activation(gate[:, cols], gate[:, cols], ACT.Copy, scale=0.5, bias=0.5).then_inc(tail_done, 1)

        @block.vector
        def _(dve):
            v = nc.vector

            def reduce_chunk(r, bank, chunks):
                h, j, _, keys, _ = PASS1[r][0]
                flat = part_max[:, h, :, :].rearrange("p t k -> p (t k)")
                at = 5 * PLACE[j]
                src = bank[:, :]
                if keys == 512:
                    dst = part_max[:, h, PLACE[j], 4:5] if j == 7 else part_max[:, h, PLACE[j], 0:1]
                elif keys == 128:
                    dst = flat[:, at + 4:at + 8]
                    src = src.rearrange("p (a c) -> p a c", c=128)
                else:
                    dst = flat[:, at:at + 22:21]
                    src = src.rearrange("p (a c) -> p a c", c=256)
                dve.wait_ge(s1_full, chunks + 1)
                v.reduce_max(dst, src, AX.X).then_inc(s1_read, 1)

            def reduce_diag(j, done):
                dve.wait_ge(diag_masked, done + 1)
                v.reduce_max(part_max[:, :, PLACE[j], 3], diag[:, j % 2, :, :], AX.X).then_inc(diag_done, 1)

            def finish_max(groups, plain, diagonal):
                dve.wait_ge(s1_read, plain)
                dve.wait_ge(diag_done, diagonal)
                v.reduce_max(q_max[:, :].rearrange("p (g b a) -> p g a b", b=2, a=2),
                             part_max[:, :, :, :].rearrange("p h (c a b) k -> p (h c) a b k", a=2, b=2),
                             AX.X).then_inc(max_ready, 1)
                dve.wait_ge(max_ready, groups + 1)

            def split_max(use, rows, steps):
                got = shared[0:GH * T, 0:128]
                dve.wait_ge(bank_full, use + 1)
                if rows is not None:
                    dve.wait_ge(rows_in, rows)
                v.tensor_scalar(neg_parts[:, 0, :], got, -1.0, None, ALU.mult).then_inc(split_step, 1)
                dve.wait_ge(split_step, steps + 1)
                v.scalar_tensor_tensor(neg_rest[:, :], got, -1.0, neg_parts[:, 0, :], ALU.mult,
                                       ALU.subtract).then_inc(bank_read, 1)
                dve.wait_ge(bank_read, use + 1)
                v.tensor_copy(neg_parts[:, 1, :], neg_rest[:, :]).then_inc(split_step, 1)
                dve.wait_ge(split_step, steps + 2)
                v.tensor_tensor(neg_parts[:, 2, :], neg_rest[:, :], neg_parts[:, 1, :], ALU.subtract).then_inc(parts_ready, 1)

            def bn(src, tiles):
                for h in tiles:
                    v.bn_stats(stats[:, h, :], src[:, h, :]).then_inc(bn_done, 1)

            def bn_end(ln):
                wait_apart(dve, bn_done, ln * (2 * T) + T)
                for h in range(T):
                    v.bn_aggr(mean_var[:, h, :], stats[:, h, :]).then_inc(bn_done, 1)
                wait_apart(dve, bn_done, ln * (2 * T) + 2 * T)
                v.tensor_scalar(var_eps[:, :], mean_var[:, :, 1], EPS, None, ALU.add).then_inc(stats_ready, 1)

            def shift_of(ln):
                dve.wait_ge(rstd_ready, ln + 1)
                v.scalar_tensor_tensor(shift[:, :], mean_var[:, :, 0], -1.0, rstd[:, :], ALU.mult,
                                       ALU.mult).then_inc(shift_ready, 1)

            def normalise_first(src, ready):
                dve.wait_ge(shift_ready, ready)
                for h in range(BY_VECTOR):
                    last = v.tensor_scalar(xn[:, h, :], src[:, h, :], rstd[:, h:h + 1], shift[:, h:h + 1],
                                           ALU.mult, ALU.add)
                last.then_inc(xn_ready, 1)

            def rest_of(n, use):
                cols = slice(HALF * (n % 2), HALF * (n % 2) + HALF)
                dst = (q_parts, k_parts)[n // 2]
                v.tensor_tensor(rest[:, n % 2, :], shared[:, :], dst[:, 0, cols], ALU.subtract).then_inc(bank_read, 1)

            def normalise_out(slot, half, use, units):
                got = shared[:, :].rearrange("p (j n c) -> p j n c", j=4, n=GH)
                dve.wait_ge(bank_full, use + 1)
                v.reciprocal(inv[:, :, :], got[:, :, :, H]).then_inc(inv_step, 1)
                dve.wait_ge(inv_step, units * 2 + 1)
                w = w_sum[:, :].rearrange("p (n j) -> p j n", j=T)[:, 4 * half:4 * half + 4, GH * slot:GH * slot + GH]
                v.tensor_tensor(inv_w[:, :, :], inv[:, :, :], w, ALU.mult).then_inc(inv_step, 1)
                dve.wait_ge(inv_step, units * 2 + 2)
                dst = att[:, :, :].rearrange("p h (n j) -> p j n h", j=T)[:, 4 * half:4 * half + 4, GH * slot:GH * slot + GH, :]
                v.tensor_tensor(dst, got[:, :, :, 0:H], inv_w[:, :, :].unsqueeze(3).broadcast_to([128, 4, GH, H]),
                                ALU.mult).then_inc(bank_read, 1)

            def join_last(batches, use):
                wait_apart(dve, joined, batches + 1)
                dve.wait_ge(bank_read, use + 1)
                v.tensor_tensor(x1[:, :, JOINED:D], att[:, :, JOINED:D], x1[:, :, JOINED:D], ALU.add).then_inc(att_ready, 1)
                wait_apart(dve, att_ready, batches + 1)

            def mix_x(side, n):
                product = (scaled, xk)[side]
                dve.wait_ge((scaled_r, scaled_k)[side], n + 1)
                for cols in halves:
                    v.scalar_tensor_tensor((xr, xk)[side][:, cols], xT[:, cols], one_less_mu[:, side:side + 1],
                                           product[:, cols], ALU.mult, ALU.add).then_inc(mixed, 1)

            def gate_v(half, use):
                cols = slice(HALF * half, HALF * half + HALF)
                dve.wait_ge(bank_full, use + 1)
                v.tensor_tensor(yT[:, cols], shared[:, :], gate[:, cols], ALU.mult).then_inc(bank_read, 1)

            def add_y(u, use, stored):
                dve.wait_ge(bank_full, use + 1)
                if u == 0:
                    dve.wait_ge(out_done, stored)
                v.tensor_tensor(y[:, 4 * u:4 * u + 4, :], shared[:, :].rearrange("p (h d) -> p h d", h=4),
                                x1[:, 4 * u:4 * u + 4, :], ALU.add).then_inc(bank_read, 1)

            v.memset(fill[:, 0:1], 0.0).then_inc(fill_ready, 1)
            v.memset(fill[:, 1:2].bitcast(BF16), 1.0).then_inc(fill_ready, 1)
            v.memset(part_max[:, :, :, :], 3 * LOW)
            v.memset(xT[:, 0:1], 0.0).then_inc(column_ready, 1)
            for u in range(2):
                dve.wait_ge(x_half_in[u], 16)
                bn(x_ln, range(4 * u, 4 * u + 4))
            bn_end(0)
            dve.wait_ge(w_in, 7 * 16)
            qkv = w_all[:, :, :].rearrange("p (g n) e -> p g e n", n=GH)
            v.tensor_copy(wq[:, :].rearrange("p (g e n) -> p g e n", e=H, n=GH), qkv[:, :, 0:H, :]).then_inc(w_ready, 1)
            v.tensor_copy(wk[:, :].rearrange("p (g e n) -> p g e n", e=H, n=GH), qkv[:, :, H:2 * H, :]).then_inc(w_ready, 1)
            v.tensor_copy(wv[:, :].rearrange("p (n h) -> p n h", h=H), w_all[:, :, 2 * H:3 * H]).then_inc(w_ready, 1)
            v.tensor_scalar(one_less_mu[:, :], mu[:, :], -1.0, 1.0, ALU.mult, ALU.add).then_inc(w_ready, 1)
            shift_of(0)
            normalise_first(x_ln, 1)
            for n in range(4):
                dve.wait_ge(hi_ready, n + 1)
                if n >= 2:
                    dve.wait_ge(lo_ready, n - 1)
                v.tensor_tensor(rest[:, n % 2, :], qk_banks[n][:, :], (q_parts, k_parts)[n // 2][:, 0, halves[n % 2]],
                                ALU.subtract).then_inc(rest_done, 1)
            for n in range(CHUNKS + AHEAD):
                r = n % CHUNKS
                if r not in ON_DIAGONAL:
                    reduce_chunk(r, bank1[n % RING], n)
                if r - DIAG_LAG in ON_DIAGONAL:
                    reduce_diag(ON_DIAGONAL.index(r - DIAG_LAG), chunks_before(n - DIAG_LAG)[0])
                if n == CHUNKS - 1:
                    finish_max(0, PLAIN, DIAG)
                if n == CHUNKS + 2:
                    split_max(0, None, 0)

            def phase(f):
                for step in range(CHUNKS):
                    ahead = f.first_pass(step)
                    if ahead:
                        groups, slot, r = ahead
                        if r not in ON_DIAGONAL:
                            reduce_chunk(r, bank1[r % RING], f.count(CHUNKS, groups * CHUNKS + r))
                        if r - DIAG_LAG in ON_DIAGONAL:
                            j = ON_DIAGONAL.index(r - DIAG_LAG)
                            reduce_diag(j, f.diagonal((groups, slot, r - DIAG_LAG)))
                        if r == CHUNKS - 1:
                            finish_max(f.count(1, groups), f.count(PLAIN, (groups + 1) * PLAIN),
                                       f.count(DIAG, (groups + 1) * DIAG))
                    name = f.steps.get(step)
                    if name == OT_LAST:
                        normalise_out((f.off - 1) % GROUPS, 1, f.use(name), f.count(2, -1))
                    elif name == OT_FIRST:
                        normalise_out(f.slot, 0, f.use(name), f.count(2, 0))
                    elif name == MAX_ROW:
                        split_max(f.use(name), f.count(48, 48), f.count(2, 2))
                    elif f.project and name and name.startswith("QK"):
                        n = int(name[2])
                        dve.wait_ge(hi_ready, f.per_round(4, 4 + n + 1))
                        dve.wait_ge(lo_ready, f.per_round(4, 4 + n - 1))
                        rest_of(n, f.use(name))
                    elif name in ("W0", "W1"):
                        dve.wait_ge(gate_ready, f.per_round(1, 0))
                        gate_v(int(name[1]), f.use(name))
                    elif name in ("Y0", "Y1"):
                        add_y(int(name[1]), f.use(name), f.per_round(16, 0))
                        v_done(f.use(name) + 1)
                    if f.mix and step == f.events["join"]:
                        join_last(f.per_round(1, 0), f.use(OT_LAST))
                    tile = step - f.events.get("stats", CHUNKS)
                    if f.project == 1:
                        if tile == 0:
                            dve.wait_ge(x_in, f.per_round(16, 16))
                        if 0 <= tile < T:
                            bn(x_ln, (tile,))
                        if tile == T:
                            bn_end(f.per_round(2, 1))
                    elif f.mix:
                        if 0 <= tile < T:
                            bn(x1, (tile,))
                        if tile == T - 1:
                            bn_end(f.per_round(2, 2))
                    if step == f.events.get("shift"):
                        shift_of(f.per_round(2, 1 if f.project else 2))
                    for side in range(2):
                        if step == f.events.get(("mix r", "mix k")[side]):
                            mix_x(side, f.per_round(1, 0))

            def v_done(use):
                dve.wait_ge(bank_read, use)
                dve.sem_inc(y_ready, 1)

            rounds(dve, phase)
            normalise_out(GROUPS - 1, 1, tail_use, 2 * B * GROUPS - 1)
            join_last(LAST_ROUND, tail_use)
            bn(x1, range(T))
            bn_end(2 * LAST_ROUND + 1)
            shift_of(2 * LAST_ROUND + 1)
            normalise_first(x1, 2 * B)
            for half, cols in enumerate(halves):
                dve.wait_ge(tail_done, 2 + half + 1)
                v.scalar_tensor_tensor(xk[:, cols], xT[:, cols], one_less_mu[:, 1:2], scaled[:, cols],
                                       ALU.mult, ALU.add).then_inc(mixed, 1)
            dve.wait_ge(scaled_k, B)
            for cols in halves:
                v.scalar_tensor_tensor(xr[:, cols], xT[:, cols], one_less_mu[:, 0:1], xr[:, cols],
                                       ALU.mult, ALU.add).then_inc(mixed, 1)
            for half, cols in enumerate(halves):
                dve.wait_ge(tail_done, 4 + half + 1)
                v.tensor_tensor(k_act[:, cols], k_relu[:, cols], k_relu[:, cols], ALU.mult).then_inc(act_ready, 1)
            for half, cols in enumerate(halves):
                dve.wait_ge(tail_done, 8 + 2 * half)
                dve.wait_ge(tail_full, 6 + half + 1)
                v.tensor_tensor(yT[:, cols], (acc, bank2[0])[half][:, :], gate[:, cols], ALU.mult).then_inc(yT_ready, 1)
            dve.wait_ge(out_done, 16 * B)
            for u in range(2):
                dve.wait_ge(tail_full, 8 + u + 1)
                v.tensor_tensor(y[:, 4 * u:4 * u + 4, :], bank2[1 + u][:, :].rearrange("p (h d) -> p h d", h=4),
                                x1[:, 4 * u:4 * u + 4, :], ALU.add).then_inc(y_ready, 1)

        @block.tensor
        def _(pe):
            mm = nc.tensor.matmul

            def first_pass(slot, r, bank):
                for h, j, k0, n, at in PASS1[r]:
                    last = mm(bank[:, at:at + n], qa[0:QK_ROWS, slot, h, 128 * j:128 * j + 128],
                              ka[0:QK_ROWS, slot, h, k0:k0 + n], start=True, stop=True)
                last.then_inc(s1_full, 1)

            def second_pass(slot, c, bank):
                for h, i, q0, n, at in PASS2[c]:
                    last = mm(bank[:, at:at + n], ka[0:ALL_ROWS, slot, h, 128 * i:128 * i + 128],
                              qa[0:ALL_ROWS, slot, h, q0:q0 + n], start=True, stop=True)
                last.then_inc(s2_full, 1)

            def values(slot, k):
                pieces = pieces_of_set(k)
                for i, q0, n, heads in pieces:
                    at = q0 % HALF
                    for h, c, place in heads:
                        last = mm(acc[VW * h:VW * h + VW, at:at + n], va[:, slot, i, h, :],
                                  probs[:, c % PSLOTS, place:place + n], start=i == 0,
                                  stop=k in (HALF_SETS - 1, SETS - 1))
                last.then_inc(sets_done, 1)

            def transpose_out():
                for j in range(4):
                    last = nc.tensor.transpose(shared[:, 128 * j:128 * j + 128], oT[:, 128 * j:128 * j + 128], ident[:, :])
                last.then_inc(bank_full, 1)

            def transpose_max():
                nc.tensor.transpose(shared[0:GH * T, 0:128], q_max[:, :], ident[:, :]).then_inc(bank_full, 1)

            def transpose_x(u, bank):
                for h in range(4):
                    last = nc.tensor.transpose(bank[:, 128 * h:128 * h + 128], xn[:, 4 * u + h, :], ident[:, :])
                return last

            def project_qk(n, bank):
                return mm(bank[:, :], (wq, wk)[n // 2][:, :], xT[:, 1 + HALF * (n % 2):1 + HALF * (n % 2) + HALF],
                          start=True, stop=True)

            def project_v(u, bank):
                for t in range(4):
                    at = 1 + 128 * (4 * u + t)
                    last = mm(bank[:, 128 * t:128 * t + 128], xT[:, at:at + 128], wv[:, :], start=True, stop=True)
                return last

            def mix_product(n, src, half, bank):
                return mm(bank[:, :], w_mixT[:, n, :], src[:, halves[half]], start=True, stop=True)

            def transpose_y(u, bank):
                tiles = yT[:, :].rearrange("d (p h) -> d h p", h=T)
                for h in range(4):
                    last = nc.tensor.transpose(bank[:, 128 * h:128 * h + 128], tiles[:, 4 * u + h, :], ident[:, :])
                return last

            def keep_warm(products):
                for _ in range(products):
                    mm(bank2[RING - 1][:, 0:128], ident[:, :], ident[:, :], start=True, stop=True)

            pe.wait_ge(consts_ready, 2)
            keep_warm(WARM[0])
            pe.wait_ge(xn_ready, 2)
            for u in range(2):
                transpose_x(u, (bank2[2], acc)[u]).then_inc(setup_full, 1)
            pe.wait_ge(w_ready, 4)
            pe.wait_ge(column_ready, 1)
            pe.wait_ge(setup_copied, 2)
            for n in range(4):
                project_qk(n, qk_banks[n]).then_inc(setup_full, 1)
            for u in range(2):
                project_v(u, bank2[u]).then_inc(setup_full, 1)
            pe.wait_ge(w_in, 7 * 16)
            mm(bank2[2][:, 0:D], ones[:, :], wo[:, :], start=True, stop=True).then_inc(setup_full, 1)
            for n in range(3):
                last = nc.tensor.transpose(acc[:, 128 * n:128 * n + 128], w_mix[:, n, :], ident[:, :])
            last.then_inc(setup_full, 1)
            for n in range(CHUNKS + AHEAD):
                if n % CHUNKS == 0:
                    pe.wait_ge(qk_in[n // CHUNKS], 16 * QK_DMAS)
                if n < RING:
                    pe.wait_ge(rest_done, n + 1)
                elif (n - RING) % CHUNKS in ON_DIAGONAL:
                    pe.wait_ge(diag_copied, chunks_before(n - RING)[0] + 1)
                else:
                    pe.wait_ge(s1_read, chunks_before(n - RING)[1] + 1)
                first_pass(n // CHUNKS, n % CHUNKS, bank1[n % RING])
                if n == CHUNKS + 2:
                    pe.wait_ge(max_ready, 1)
                    pe.wait_ge(rest_done, 4)
                    transpose_max()

            def phase(f):
                for step in range(CHUNKS):
                    if step == 0:
                        pe.wait_ge(rows_in, f.count(48, 48))
                    if f.last and step >= RING:
                        if step < 2 * RING:
                            pe.wait_ge(s1_read, PLAIN * B * GROUPS)
                        else:
                            pe.wait_ge(exp_done, f.count(CHUNKS, step + 1 - 2 * RING))
                    elif f.first and step < RING:
                        pe.wait_ge(setup_copied, 3 + step)
                    else:
                        pe.wait_ge(exp_done, f.count(CHUNKS, step + 1 - RING))
                    second_pass(f.slot, step, banks_for_second(f)[step])
                    ahead = f.first_pass(step)
                    if ahead:
                        groups, slot, r = ahead
                        if r == 0:
                            pe.wait_ge(qk_in[slot], f.fills(groups))
                        before = groups, slot, r - RING
                        if (r - RING) % CHUNKS in ON_DIAGONAL:
                            pe.wait_ge(diag_copied, f.diagonal(before) + 1)
                        else:
                            pe.wait_ge(s1_read, f.plain(before) + 1)
                        first_pass(slot, r, bank1[r % RING])
                    lag = LAG + LATER * f.last
                    if step - lag in SET_ENDS:
                        k = SET_ENDS.index(step - lag)
                        end = SET_ENDS[k]
                        pe.wait_ge(exp_done, f.count(CHUNKS, end + 1))
                        if end in DIAGONAL:
                            pe.wait_ge(masked, f.count(MASKS, masks_until(end)))
                        if k == 0:
                            pe.wait_ge(v_ready, f.count(1, 1))
                        if f.first and k == 0:
                            pe.wait_ge(setup_copied, 6)
                        elif k in (0, HALF_SETS):
                            pe.wait_ge(acc_read, f.count(2, int(k > 0)))
                        values(f.slot, k)
                    elif step - LAG + CHUNKS in SET_ENDS and not f.first:
                        k = SET_ENDS.index(step - LAG + CHUNKS)
                        end = SET_ENDS[k]
                        pe.wait_ge(exp_done, f.count(CHUNKS, end + 1 - CHUNKS))
                        pe.wait_ge(masked, f.count(MASKS, masks_until(end) - MASKS))
                        values((f.off - 1) % GROUPS, k)
                    name = f.steps.get(step)
                    if not name:
                        continue
                    pe.wait_ge(bank_read, f.use(name))
                    if name == OT_LAST:
                        pe.wait_ge(acc_read, f.count(2, 0))
                        transpose_out()
                        continue
                    if name == OT_FIRST:
                        pe.wait_ge(acc_read, f.count(2, 1))
                        transpose_out()
                        continue
                    if name == MAX_ROW:
                        pe.wait_ge(max_ready, f.count(1, 2))
                        transpose_max()
                        continue
                    n = int(name[-1])
                    if name in ("XT0", "XT1"):
                        pe.wait_ge(xn_ready, f.per_round(4, 4 if f.project else 6))
                        last = transpose_x(n, shared)
                    elif name.startswith("QK"):
                        last = project_qk(n, shared)
                    elif name in ("V0", "V1"):
                        last = project_v(n, shared)
                    elif name in ("R0", "R1"):
                        pe.wait_ge(mixed, f.per_round(4, n + 1))
                        last = mix_product(0, xr, n, shared)
                    elif name in ("K0", "K1"):
                        pe.wait_ge(mixed, f.per_round(4, 2 + n + 1))
                        last = mix_product(1, xk, n, shared)
                    elif name in ("W0", "W1"):
                        pe.wait_ge(act_ready, f.per_round(2, n - 1))
                        last = mix_product(2, k_act, n, shared)
                    else:
                        last = transpose_y(n, shared)
                    last.then_inc(bank_full, 1)

            rounds(pe, phase)
            for k in (SETS - 2, SETS - 1):
                pe.wait_ge(exp_done, CHUNKS * (B * GROUPS - 1) + SET_ENDS[k] + 1)
                pe.wait_ge(masked, MASKS * (B * GROUPS - 1) + masks_until(SET_ENDS[k]))
                values(GROUPS - 1, k)
            pe.wait_ge(acc_read, 2 * B * GROUPS)
            pe.wait_ge(bank_read, tail_use)
            transpose_out()
            keep_warm(WARM[1])
            pe.wait_ge(xn_ready, 4 * B)
            for u in range(2):
                transpose_x(u, bank2[u]).then_inc(tail_full, 1)
            keep_warm(WARM[2])
            for half in range(2):
                pe.wait_ge(mixed, 4 * LAST_ROUND + half + 1)
                mix_product(1, xk, half, bank1[1 + half]).then_inc(tail_full, 1)
            for half in range(2):
                pe.wait_ge(mixed, 4 * LAST_ROUND + 2 + half + 1)
                mix_product(0, xr, half, (bank2[2], bank1[0])[half]).then_inc(tail_full, 1)
            for half in range(2):
                pe.wait_ge(act_ready, 2 * LAST_ROUND + half + 1)
                mix_product(2, k_act, half, (acc, bank2[0])[half]).then_inc(tail_full, 1)
            pe.wait_ge(yT_ready, 2)
            for u in range(2):
                transpose_y(u, bank2[1 + u]).then_inc(tail_full, 1)


def kernel(**inputs):
    import numpy as np
    import concourse.bacc as bacc
    from concourse.bass_utils import run_bass_kernel_spmd

    names = ["L0_attn_x", "L0_attn_W_qkv", "L0_attn_W_out", "L0_ffn_W_r", "L0_ffn_W_k", "L0_ffn_W_v",
             "L0_ffn_mu_r", "L0_ffn_mu_k"]
    nc = bacc.Bacc("TRN2", target_bir_lowering=False, num_devices=1)
    arrays, args = {}, []
    for name in names:
        a = np.ascontiguousarray(inputs[name])
        arrays[f"in_{name}"] = a
        args.append(nc.dram_tensor(f"in_{name}", a.shape, mybir.dt.from_np(a.dtype), kind="ExternalInput").ap())
    args.append(nc.dram_tensor("out_x", (B, S, D), F32, kind="ExternalOutput").ap())
    build(nc, *args)
    r = run_bass_kernel_spmd(nc, [arrays], core_ids=[0])
    return r.results[0]["out_x"]
```
